# Optimizing a Trainium2 kernel written in Bass

```python
import numpy as np
import jax
import jax.numpy as jnp

def _softmax(x, axis=-1):
    return jax.nn.softmax(x, axis=axis)

def _gelu(x):
    return jax.nn.gelu(x, approximate=True)

def _silu(x):
    return jax.nn.silu(x)

def _sigmoid(x):
    return jax.nn.sigmoid(x)

def _layernorm(x, axis=-1, eps=1e-05):
    m = jnp.mean(x, axis=axis, keepdims=True)
    v = jnp.var(x, axis=axis, keepdims=True)
    return (x - m) / jnp.sqrt(v + eps)

def _scatter_add(tgt, idx, src, axis=0):
    return tgt.at[idx].add(src)

def _segment_sum(src, seg, n):
    return jax.ops.segment_sum(src, seg, n)
kernel_name = 'mk_adaln_d1_jaxref_r4_0c9ad8'

def setup_inputs(seed: int=0):
    np.random.seed(seed)
    _w = jnp.asarray

    def _L0_attn_setup():
        import jax, jax.numpy as jnp
        import numpy as np
        HEADS = 16
        HIDDEN = 256
        key = jax.random.key(seed)
        ks = jax.random.split(key, 9)
        E, H = (256, HIDDEN)
        N, L = (4, 512)
        s = 0.02
        return {'X_embed': jax.random.normal(ks[0], (N, L, E), dtype=jnp.float32), 'Wq': jax.random.normal(ks[1], (E, H), dtype=jnp.float32) * s, 'bq': jax.random.normal(ks[2], (H,), dtype=jnp.float32) * s, 'Wk': jax.random.normal(ks[3], (E, H), dtype=jnp.float32) * s, 'bk': jax.random.normal(ks[4], (H,), dtype=jnp.float32) * s, 'Wv': jax.random.normal(ks[5], (E, H), dtype=jnp.float32) * s, 'bv': jax.random.normal(ks[6], (H,), dtype=jnp.float32) * s, 'Wo': jax.random.normal(ks[7], (H, H), dtype=jnp.float32) * s, 'bo': jax.random.normal(ks[8], (H,), dtype=jnp.float32) * s}
    _L0_attn_in = _L0_attn_setup()

    def _L0_ffn_setup():
        import jax, jax.numpy as jnp
        import numpy as np
        D_MODEL = 256
        N_EXPERTS = 8
        TOP_K = 2
        LN_EPS = 1e-05
        key = jax.random.key(seed)
        ks = jax.random.split(key, 8)
        B, S, d, E = (2, 512, D_MODEL, N_EXPERTS)
        f = 2 * d
        s_in = 0.02
        return {'x': jax.random.normal(ks[0], (B, S, d), jnp.float32), 'Wg': jax.random.normal(ks[1], (d, E), jnp.float32) * s_in, 'bg': jnp.zeros((E,), jnp.float32), 'W1': jax.random.normal(ks[2], (E, d, f), jnp.float32) * s_in, 'b1': jnp.zeros((E, f), jnp.float32), 'W2': jax.random.normal(ks[3], (E, f, d), jnp.float32) * s_in, 'b2': jnp.zeros((E, d), jnp.float32), 'gamma': jnp.ones((d,), jnp.float32), 'beta': jnp.zeros((d,), jnp.float32)}
    _L0_ffn_in = _L0_ffn_setup()
    _L0_c = _w((lambda *s: np.random.randn(*s).astype(np.float32) * 0.05)(2, 256))
    _L0_wmod = _w((lambda *s: np.random.randn(*s).astype(np.float32) * 0.05)(256, 6 * 256) * 256 ** (-0.5))
    _d = {'L0_attn_X_embed': _L0_attn_in['X_embed'], 'L0_attn_Wq': _L0_attn_in['Wq'], 'L0_attn_bq': _L0_attn_in['bq'], 'L0_attn_Wk': _L0_attn_in['Wk'], 'L0_attn_bk': _L0_attn_in['bk'], 'L0_attn_Wv': _L0_attn_in['Wv'], 'L0_attn_bv': _L0_attn_in['bv'], 'L0_attn_Wo': _L0_attn_in['Wo'], 'L0_attn_bo': _L0_attn_in['bo'], 'L0_ffn_Wg': _L0_ffn_in['Wg'], 'L0_ffn_bg': _L0_ffn_in['bg'], 'L0_ffn_W1': _L0_ffn_in['W1'], 'L0_ffn_b1': _L0_ffn_in['b1'], 'L0_ffn_W2': _L0_ffn_in['W2'], 'L0_ffn_b2': _L0_ffn_in['b2'], 'L0_ffn_gamma': _L0_ffn_in['gamma'], 'L0_ffn_beta': _L0_ffn_in['beta'], 'L0_c': _L0_c, 'L0_wmod': _L0_wmod}
    _x0 = _d['L0_attn_X_embed']
    _d['L0_attn_X_embed'] = jax.random.normal(jax.random.fold_in(jax.random.key(seed), 1), (2, 4096, 256), dtype=_x0.dtype)
    del _x0
    return _d

def reference(L0_attn_X_embed, L0_attn_Wq, L0_attn_bq, L0_attn_Wk, L0_attn_bk, L0_attn_Wv, L0_attn_bv, L0_attn_Wo, L0_attn_bo, L0_ffn_Wg, L0_ffn_bg, L0_ffn_W1, L0_ffn_b1, L0_ffn_W2, L0_ffn_b2, L0_ffn_gamma, L0_ffn_beta, L0_c, L0_wmod):

    def _L0_attn_ref(X_embed, Wq, bq, Wk, bk, Wv, bv, Wo, bo):
        import jax, jax.numpy as jnp
        import numpy as np
        HEADS = 16
        HIDDEN = 256
        N, L, _ = X_embed.shape
        H, heads = (HIDDEN, HEADS)
        dh = H // heads
        Q = X_embed @ Wq + bq
        K = X_embed @ Wk + bk
        V = X_embed @ Wv + bv
        Q = Q.reshape(N, heads, L, dh)
        K = K.reshape(N, heads, L, dh)
        V = V.reshape(N, heads, L, dh)
        scale = np.float32(1.0 / np.sqrt(H))
        Q = Q * scale
        K = K * scale
        scores = jnp.einsum('neax,nebx->neab', Q, K)
        A = jax.nn.softmax(scores, axis=2)
        Out = jnp.einsum('neab,neax->neax', A, V)
        Out = Out.reshape(N, L, H)
        return Out @ Wo + bo

    def _L0_ffn_ref(x, Wg, bg, W1, b1, W2, b2, gamma, beta):
        import jax, jax.numpy as jnp
        import numpy as np
        D_MODEL = 256
        N_EXPERTS = 8
        TOP_K = 2
        LN_EPS = 1e-05
        logits = jnp.einsum('bsd,de->bse', x, Wg) + bg
        topk_vals, topk_idx = jax.lax.top_k(logits, TOP_K)
        topk_w = jax.nn.softmax(topk_vals, axis=-1)
        h = jax.nn.relu(jnp.einsum('bsd,edf->bsef', x, W1) + b1)
        eo = jnp.einsum('bsef,efd->bsed', h, W2) + b2
        sel = jnp.take_along_axis(eo, topk_idx[..., None], axis=2)
        mixed = jnp.sum(sel * topk_w[..., None], axis=2)
        y = mixed + x
        mu = jnp.mean(y, axis=-1, keepdims=True)
        var = jnp.mean(jnp.square(y - mu), axis=-1, keepdims=True)
        return gamma * (y - mu) * jax.lax.rsqrt(var + LN_EPS) + beta
    x = L0_attn_X_embed
    mod = (_silu(L0_c) @ L0_wmod).reshape(L0_c.shape[0], 6, 1, -1)
    sa, ca, ga, sb, cb, gb = (mod[:, 0], mod[:, 1], mod[:, 2], mod[:, 3], mod[:, 4], mod[:, 5])
    ga = (2 * (ga >= 0) - 1) * jnp.maximum(jnp.abs(ga), 0.25)
    gb = (2 * (gb >= 0) - 1) * jnp.maximum(jnp.abs(gb), 0.25)
    h = _layernorm(x, axis=-1) * (1 + ca) + sa
    x = x + ga * _L0_attn_ref(h, L0_attn_Wq, L0_attn_bq, L0_attn_Wk, L0_attn_bk, L0_attn_Wv, L0_attn_bv, L0_attn_Wo, L0_attn_bo)
    h = _layernorm(x, axis=-1) * (1 + cb) + sb
    x = x + gb * _L0_ffn_ref(h, L0_ffn_Wg, L0_ffn_bg, L0_ffn_W1, L0_ffn_b1, L0_ffn_W2, L0_ffn_b2, L0_ffn_gamma, L0_ffn_beta)
    return x

_drawn_inputs = setup_inputs


def setup_inputs(seed=0):
    import zlib

    import numpy as np

    out = dict(_drawn_inputs(seed))
    spreads = {'L0_ffn_bg': (0.0, 0.67),
     'L0_ffn_b1': (0.0, 0.8),
     'L0_ffn_b2': (0.0, 0.454),
     'L0_ffn_gamma': (1.0, 0.2),
     'L0_ffn_beta': (0.0, 0.337)}
    factors = {'L0_attn_Wq': 64.0,
     'L0_attn_bq': 187.906,
     'L0_attn_Wk': 64.0,
     'L0_attn_bk': 200.0,
     'L0_attn_bv': 26.515,
     'L0_attn_bo': 8.0,
     'L0_ffn_W1': 3.785,
     'L0_ffn_W2': 3.044}
    for name, (base, spread) in spreads.items():
        noise = np.random.default_rng([zlib.crc32(name.encode()), seed]).standard_normal(out[name].shape)
        drawn = base * np.exp(spread * noise) if base else spread * noise
        out[name] = jnp.asarray(drawn.astype(out[name].dtype))
    for name, factor in factors.items():
        out[name] = (out[name] * factor).astype(out[name].dtype)
    return out
```

```python
from contextlib import ExitStack

import concourse.bass as bass
from concourse import mybir

F32 = mybir.dt.float32
BF16 = mybir.dt.bfloat16
ALU = mybir.AluOpType
ACT = mybir.ActivationFunctionType
AX = mybir.AxisListType

P = 128
ROWS = 256
D = 256
DH = 16
GROUPS = D // DH
POS = ROWS * GROUPS
CHUNK = 1024
NCHUNK = POS // CHUNK
TILES = POS // P
NE = 8
FF = 512
NF = FF // P
NB = 2
BLOCKS = NB * 4096 // ROWS
EPS = 1e-5
SLOTS = NCHUNK * TILES

HEAD = ((0, 2), (2, 3), (5, 3))
BODY_FIRST = 8
BODY_ITERS = 4
BATCHES = len(HEAD) + 2 * BODY_ITERS

HI, MID, LO = range(3)
TERMS = ((HI, HI), (HI, MID), (MID, HI), (HI, LO), (LO, HI), (MID, MID), (MID, LO), (LO, MID))

PRE_PIECES = ("h1T", "Q", "K", "V")
HEAD_PIECES = ("Wo", "h1T", "Q", "K", "h2T", "logits", "V", "gT", "b2")
POST_PIECES = tuple(k for k in HEAD_PIECES if k not in PRE_PIECES)
EXPERT_PIECES = ("F01", "F23", "Y")
PER_BLOCK = len(HEAD_PIECES) + NE * len(EXPERT_PIECES)


GATE_LINKS = 8
SPLIT_LINKS = 3
CONST_LOADS = 19


def piece_no(i, kind, e=0):
    fixed = isinstance(i, int)
    if fixed and i < 1:
        return len(PRE_PIECES) * (i + 1) + PRE_PIECES.index(kind)
    base = 2 * len(PRE_PIECES) + PER_BLOCK * (i - 1)
    kinds = HEAD_PIECES
    if fixed and i >= BLOCKS - 1:
        kinds = POST_PIECES
        base = base - (len(PRE_PIECES) if i >= BLOCKS else 0)
    if kind in EXPERT_PIECES:
        return base + len(kinds) + len(EXPERT_PIECES) * e + EXPERT_PIECES.index(kind)
    return base + kinds.index(kind)


def adaln_layer(nc, x, Wq, bq, Wk, bk, Wv, bv, Wo, bo, Wg, bg, W1, b1, W2, b2, gamma, beta, c, wmod, out):
    with ExitStack() as ctx:
        def sb(name, shape, dt=F32):
            return ctx.enter_context(nc.sbuf_tensor(name, shape, dt))

        def ps(name, shape):
            return ctx.enter_context(nc.psum_tensor(name, shape, F32))

        def sem(name):
            return ctx.enter_context(nc.semaphore(name))

        E = [[sb(f"E{s}{j}", [P, POS]) for j in range(3)] for s in range(2)]
        qT = [sb(f"qT{s}", [P, POS], BF16) for s in range(2)]
        kT = [sb(f"kT{s}", [P, POS], BF16) for s in range(2)]
        wsum = [sb(f"wsum{s}", [P, 3, NCHUNK, 2, 32]) for s in range(2)]
        xin = sb("xin", [P, 2, D])
        h1T = sb("h1T", [P, 2, ROWS])
        qf = sb("qf", [P, 2, ROWS])
        kf = sb("kf", [P, 2, ROWS])
        qparts = sb("qparts", [P, 3, 2, ROWS], BF16)
        kparts = sb("kparts", [P, 3, 2, ROWS], BF16)
        vT = [sb(f"vT{s}", [P, 2, ROWS]) for s in range(2)]
        x1 = [sb(f"x1{s}", [P, 2, D]) for s in range(2)]
        ao = sb("ao", [P, 2, D])
        h2 = sb("h2", [P, 2, D])
        h2T = sb("h2T", [P, 2, ROWS])
        y = sb("y", [P, 2, D])
        w1s = sb("w1s", [P, 2, FF])
        w2s = sb("w2s", [P, NF, D])
        hid = sb("hid", [P, NF, ROWS])
        wq_s, wk_s, wv_s, wo_s = (sb(n, [P, 2, D]) for n in ("wq_s", "wk_s", "wv_s", "wo_s"))
        wg_s = sb("wg_s", [P, 2, NE])
        b2_s = sb("b2_s", [NE, D])
        ident = sb("ident", [P, P])
        earlier = sb("earlier", [P, NE, NE])
        mod_names = ("sa", "c1a", "ga", "sb", "c1b", "gb")
        sa_r, c1a_r, ga_r, sb_r, c1b_r, gscale_r = (sb(f"{n}_r", [P, NB, D]) for n in mod_names)
        gabo_r = sb("gabo_r", [P, NB, D])
        gshift_r = sb("gshift_r", [P, NB, D])
        bg_r = sb("bg_r", [P, NE])
        bq_c, bk_c, bv_c = (sb(n, [P, 2]) for n in ("bq_c", "bk_c", "bv_c"))
        b1_c = sb("b1_c", [P, NE, NF])
        nmax = [sb(f"nmax{s}", [P, 3, NCHUNK]) for s in range(2)]
        zc = [sb(f"zc{s}", [P, 3, NCHUNK]) for s in range(2)]
        nall = [sb(f"nall{s}", [P, 3]) for s in range(2)]
        dmax = [sb(f"dmax{s}", [P, 3, NCHUNK]) for s in range(2)]
        emax = [sb(f"emax{s}", [P, 3, NCHUNK]) for s in range(2)]
        zz = [sb(f"zz{s}", [P, 3, NCHUNK]) for s in range(2)]
        zsum = [sb(f"zsum{s}", [P, 3]) for s in range(2)]
        rz = [sb(f"rz{s}", [P, 3]) for s in range(2)]
        wc = [sb(f"wc{s}", [P, 3, NCHUNK]) for s in range(2)]
        ln = {n: (sb(f"st_{n}", [P, 2, 6]), sb(f"mv_{n}", [P, 2, 2]), sb(f"ve_{n}", [P, 2]), sb(f"rs_{n}", [P, 2]))
              for n in ("one", "two", "out")}
        mhalf = sb("mhalf", [P, 2])
        lg = sb("lg", [P, 2, NE])
        top = sb("top", [P, 2])
        lgd = sb("lgd", [P, 2, NE])
        lge = sb("lge", [P, 2, NE])
        gt = sb("gt", [P, 2, NE, NE])
        eq = sb("eq", [P, 2, NE, NE])
        rank = sb("rank", [P, 2, NE])
        chosen = sb("chosen", [P, 2, NE])
        gsum = sb("gsum", [P, 2])
        grec = sb("grec", [P, 2])
        gate = sb("gate", [P, 2, NE])
        gT = sb("gT", [NE, ROWS])

        S = [ps(f"S{n}", [P, 2, 512]) for n in range(3)]
        R = ps("R", [P, 2, ROWS])
        M = ps("M", [P, 2, ROWS])

        q_dram = nc.dram_tensor("q_dram", [3, GROUPS, DH, ROWS], BF16, kind="Internal").ap()
        k_dram = nc.dram_tensor("k_dram", [3, GROUPS, DH, ROWS], BF16, kind="Internal").ap()

        wmod_s = E[0][0][:, 0:2 * 1536].rearrange("p (k n) -> p k n", k=2)
        cT = E[0][1][:, 0:4].rearrange("p (k b) -> p k b", k=2)
        csig = E[0][1][:, 8:12].rearrange("p (k b) -> p k b", k=2)
        csil = E[0][1][:, 16:20].rearrange("p (k b) -> p k b", k=2)
        cwide = E[0][1][:, 1024:1024 + 4 * P].rearrange("p (k b m) -> p k b m", k=2, b=2)
        modr = [E[0][2][:, 0:1536], E[0][2][:, 1536:3072]]
        bo_r = E[1][0][:, 0:D]
        gamma_r = E[1][0][:, D:2 * D]
        beta_r = E[1][0][:, 2 * D:3 * D]
        scr = E[1][1][:, 0:2 * D].rearrange("p (b d) -> p b d", b=2)
        scr2 = E[1][1][:, 2 * D:4 * D].rearrange("p (b d) -> p b d", b=2)
        scr3 = E[1][1][:, 4 * D:6 * D].rearrange("p (b d) -> p b d", b=2)

        waits_passed = sem("waits_passed")
        consts_in = sem("consts_in")
        x_in, x1_in, w1_in, w2_in = sem("x_in"), sem("x1_in"), sem("w1_in"), sem("w2_in")
        q_parts_out, k_parts_out, qk_in, stored = sem("q_parts_out"), sem("k_parts_out"), sem("qk_in"), sem("stored")
        consts_ready = sem("consts_ready")
        ident_zeroed = sem("ident_zeroed")
        c_exp, c_silu, c_link = sem("c_exp"), sem("c_silu"), sem("c_link")
        mod_ready, mod_taken, mod_link, rows_ready = sem("mod_ready"), sem("mod_taken"), sem("mod_link"), sem("rows_ready")
        scores_ready, max_ready, exp_done = sem("scores_ready"), sem("max_ready"), sem("exp_done")
        nall_ready, dmax_ready, emax_ready, zz_ready = sem("nall_ready"), sem("dmax_ready"), sem("emax_ready"), sem("zz_ready")
        zsum_ready, rz_ready, wc_ready, wsum_ready = sem("zsum_ready"), sem("rz_ready"), sem("wc_ready"), sem("wsum_ready")
        r_batch_done, r_taken = sem("r_batch_done"), sem("r_taken")
        m_ready, m_taken = sem("m_ready"), sem("m_taken")
        stats = {n: (sem(f"bn_{n}"), sem(f"mean_ready_{n}"), sem(f"ve_ready_{n}"), sem(f"rstd_ready_{n}"),
                     sem(f"norm_ready_{n}")) for n in ("one", "two", "out")}
        h1_link, h1_ready = sem("h1_link"), sem("h1_ready")
        h2_link, h2_ready = sem("h2_link"), sem("h2_ready")
        q_link, k_link, q_split, k_split = sem("q_link"), sem("k_link"), sem("q_split"), sem("k_split")
        x1_biased, x1_ready = sem("x1_biased"), sem("x1_ready")
        gate_link, lgd_ready, lge_ready, gate_ready = sem("gate_link"), sem("lgd_ready"), sem("lge_ready"), sem("gate_ready")
        out_link, out_ready = sem("out_link"), sem("out_ready")

        def due(count):
            return not isinstance(count, int) or count > 0

        def on_its_own(eng, count):
            if not isinstance(count, int):
                eng.sem_inc(waits_passed, 1)

        class Chain:
            def __init__(self, eng, s, done):
                self.eng, self.sem, self.done = eng, s, done

            def __call__(self, ins):
                self.done = self.done + 1
                ins.then_inc(self.sem, 1)
                self.eng.wait_ge(self.sem, self.done)
                on_its_own(self.eng, self.done)

        def over_blocks(eng, block):
            block(0, 0, pre=True, att=True, post=False)
            with eng.Fori(0, (BLOCKS - 2) // 2) as pair:
                block(2 * pair + 1, 1, pre=True, att=True, post=True)
                block(2 * pair + 2, 0, pre=True, att=True, post=True)
            block(BLOCKS - 1, 1, pre=False, att=True, post=True)
            block(BLOCKS, 0, pre=False, att=False, post=True)

        def batch_index(i, b):
            return BATCHES * i + b

        def set_of(parity, b):
            return (parity + b) % 2

        def score_buffer(first, slot):
            at = NCHUNK * (first if isinstance(first, int) else BODY_FIRST) + slot
            return at % 3

        def tile_cols(tile):
            return bass.ts(tile, P)

        x_blocks = x.rearrange("b (n t p) d -> (b n) p t d", t=2, p=P)
        out_blocks = out.rearrange("b (n t p) d -> (b n) p t d", t=2, p=P)

        def rows_of_batch(rows, i):
            return rows[:, i // (BLOCKS // NB), :].unsqueeze(1).to_broadcast([P, 2, D])

        block = ctx.enter_context(nc.Block())

        @block.sync
        def _(sp):
            loads = [0]

            def cload(dst, src):
                loads[0] += 1
                sp.dma_start(dst, src, allow_slow_non_contiguous=True).then_inc(consts_in, 16)

            sp.dma_start(xin[:, :, :], x_blocks[0]).then_inc(x_in, 16)
            cload(wmod_s, wmod.rearrange("(k p) n -> p k n", p=P))
            for b in range(NB):
                for k in range(2):
                    cload(cT[:, k, b:b + 1], c[b:b + 1, k * P:(k + 1) * P].rearrange("b p -> p b"))
            for dst, src in ((wq_s, Wq), (wk_s, Wk), (wv_s, Wv), (wo_s, Wo), (wg_s, Wg)):
                cload(dst[:, :, :], src.rearrange("(k p) n -> p k n", p=P))
            cload(b2_s[:, :], b2)
            for dst, src, n in ((bo_r, bo, D), (gamma_r, gamma, D), (beta_r, beta, D), (bg_r[:, :], bg, NE)):
                cload(dst, src.rearrange("(a n) -> a n", a=1).to_broadcast([P, n]))
            for dst, src in ((bq_c, bq), (bk_c, bk), (bv_c, bv)):
                cload(dst[:, :], src.rearrange("(k p) -> p k", p=P))
            cload(b1_c[:, :, :], b1.rearrange("e (f p) -> p e f", p=P))

            def load_expert_up(e):
                sp.dma_start(w1s[:, :, :], W1[e].rearrange("(k p) f -> p k f", p=P)).then_inc(w1_in, 16)

            def load_expert_down(e):
                sp.dma_start(w2s[:, :, :], W2[e].rearrange("(f p) n -> p f n", p=P)).then_inc(w2_in, 16)

            assert loads[0] == CONST_LOADS, loads
            load_expert_up(0)
            load_expert_down(0)

            def move_parts(n, parity):
                if due(n):
                    sp.wait_ge(qk_in, 16 * 2 * len(TERMS) * n)
                    on_its_own(sp, n)
                sp.wait_ge(q_split, n + 1)
                on_its_own(sp, n + 1)
                sp.dma_start(q_dram.rearrange("s (t g) d r -> (g d) s t r", t=2), qparts[:, :, :, :]).then_inc(q_parts_out, 16)
                sp.wait_ge(k_split, n + 1)
                on_its_own(sp, n + 1)
                sp.dma_start(k_dram.rearrange("s (t g) d r -> (g d) s t r", t=2), kparts[:, :, :, :]).then_inc(k_parts_out, 16)
                if due(SLOTS * (n - 1)):
                    sp.wait_ge(scores_ready, SLOTS * (n - 1))
                    on_its_own(sp, SLOTS * (n - 1))
                sp.wait_ge(q_parts_out, 16 * (n + 1))
                on_its_own(sp, 16 * (n + 1))
                sp.wait_ge(k_parts_out, 16 * (n + 1))
                on_its_own(sp, 16 * (n + 1))
                for t, (a, b) in enumerate(TERMS):
                    strip = slice(DH * t, DH * (t + 1))
                    for dst, src, part in ((qT, q_dram, a), (kT, k_dram, b)):
                        sp.dma_start(dst[parity][strip, :].rearrange("d (g r) -> d g r", g=GROUPS),
                                     src[part].rearrange("g d r -> d g r")).then_inc(qk_in, 16)

            move_parts(0, 0)

            def sp_block(i, parity, pre, att, post):
                if pre:
                    sp.dma_start(xin[:, :, :], x_blocks[i + 1]).then_inc(x_in, 16)
                if post:
                    sp.dma_start(x1[1 - parity][:, :, :], x_blocks[i - 1]).then_inc(x1_in, 16)
                if pre:
                    move_parts(i + 1, 1 - parity)
                if post:
                    def refill(e_done, e_next):
                        sp.wait_ge(m_ready, piece_no(i, "F23", e_done) + 1)
                        on_its_own(sp, piece_no(i, "F23", e_done) + 1)
                        load_expert_up(e_next)
                        sp.wait_ge(m_ready, piece_no(i, "Y", e_done) + 1)
                        on_its_own(sp, piece_no(i, "Y", e_done) + 1)
                        load_expert_down(e_next)

                    with sp.Fori(0, BODY_ITERS - 1) as it:
                        refill(2 * it, 2 * it + 1)
                        refill(2 * it + 1, 2 * it + 2)
                    refill(NE - 2, NE - 1)
                    if att:
                        refill(NE - 1, 0)
                    sp.wait_ge(out_ready, i)
                    on_its_own(sp, i)
                    sp.dma_start(out_blocks[i - 1], y[:, :, :]).then_inc(stored, 16)
                    sp.wait_ge(stored, 16 * i)
                    on_its_own(sp, i)

            over_blocks(sp, sp_block)
            sp.wait_ge(q_parts_out, 16 * BLOCKS)
            sp.wait_ge(k_parts_out, 16 * BLOCKS)

        @block.tensor
        def _(pe):
            def piece(i, kind, e, emit):
                if due(piece_no(i, kind, e)):
                    pe.wait_ge(m_taken, piece_no(i, kind, e))
                emit().then_inc(m_ready, 1)

            def transposes(dst, src):
                for k in range(2):
                    for t in range(2):
                        last = pe.transpose(dst[:, k, t * P:(t + 1) * P], src[:, t, k * P:(k + 1) * P], ident[:, :])
                return last

            def project(w, src):
                for m in range(2):
                    for k in range(2):
                        last = pe.matmul(M[:, m, :], w[:, k, m * P:(m + 1) * P], src[:, k, :], start=(k == 0), stop=(k == 1))
                return last

            def by_tokens(src, w, n, cols):
                for t in range(2):
                    for k in range(n):
                        last = pe.matmul(M[:, t, 0:cols], src[:, k, t * P:(t + 1) * P], w[:, k, :], start=(k == 0), stop=(k == n - 1))
                return last

            def pre_piece(i, kind):
                if kind == "h1T":
                    pe.wait_ge(h1_ready, i + 2)
                    piece(i, kind, 0, lambda: transposes(M, xin))
                else:
                    pe.wait_ge(m_taken, piece_no(i, "h1T") + 1)
                    w = {"Q": wq_s, "K": wk_s, "V": wv_s}[kind]
                    piece(i, kind, 0, lambda: project(w, h1T))

            def post_piece(i, kind, parity):
                if kind == "Wo":
                    pe.wait_ge(r_taken, i)
                    piece(i, kind, 0, lambda: by_tokens(vT[1 - parity], wo_s, 2, D))
                elif kind == "h2T":
                    pe.wait_ge(h2_ready, i)
                    piece(i, kind, 0, lambda: transposes(M, h2))
                elif kind == "logits":
                    pe.wait_ge(m_taken, piece_no(i, "h2T") + 1)
                    piece(i, kind, 0, lambda: by_tokens(h2T, wg_s, 2, NE))
                elif kind == "gT":
                    pe.wait_ge(gate_ready, i)
                    def gates_transposed():
                        for t in range(2):
                            last = pe.transpose(M[0:NE, 0, t * P:(t + 1) * P], gate[:, t, :], ident[:, :])
                        return last
                    piece(i, kind, 0, gates_transposed)
                elif kind == "b2":
                    pe.wait_ge(m_taken, piece_no(i, "gT") + 1)
                    def gated_bias():
                        for t in range(2):
                            last = pe.matmul(M[:, t, :], gT[:, t * P:(t + 1) * P], b2_s[:, :], start=True, stop=True)
                        return last
                    piece(i, kind, 0, gated_bias)

            def expert_piece(i, kind, e):
                def up(pair):
                    for f in (2 * pair, 2 * pair + 1):
                        for k in range(2):
                            last = pe.matmul(M[:, f % 2, :], w1s[:, k, f * P:(f + 1) * P], h2T[:, k, :], start=(k == 0), stop=(k == 1))
                    return last
                if kind == "Y":
                    pe.wait_ge(w2_in, 16 * (NE * (i - 1) + e + 1))
                    pe.wait_ge(m_taken, piece_no(i, "F23", e) + 1)
                    piece(i, kind, e, lambda: by_tokens(hid, w2s, NF, D))
                else:
                    pe.wait_ge(w1_in, 16 * (NE * (i - 1) + e + 1))
                    piece(i, kind, e, lambda: up(0 if kind == "F01" else 1))

            def scores(i, first, slot, parity):
                n = SLOTS * i + NCHUNK * first + slot
                at_start = isinstance(first, int) and first == 0 and slot < 2
                if due(n - 1 if at_start else n - 2):
                    pe.wait_ge(exp_done, n - 1 if at_start else n - 2)
                tile = first + slot // NCHUNK
                for h in range(2):
                    q0 = (slot % NCHUNK) * CHUNK + h * 512
                    last = pe.matmul(S[score_buffer(first, slot)][:, h, :], kT[parity][:, tile_cols(tile)],
                                     qT[parity][:, q0:q0 + 512], start=True, stop=True)
                last.then_inc(scores_ready, 1)

            def weighted(exps, w, j, half, opens, closes):
                for e in range(2):
                    for q in range(4):
                        a0 = ((4 * half + q) * 2 + e) * ROWS
                        last = pe.matmul(R[32 * q:32 * q + 32, half, :], w[:, j, 2 * half + q // 2, e, :],
                                         exps[j][:, a0:a0 + ROWS], start=(opens and half == 0 and e == 0),
                                         stop=(closes and e == 1), skip_group_check=True)
                return last

            def weighted_batch(B, tiles, bset, opens, closes, per_slot, slot):
                groups = [(j, half) for j in range(tiles) for half in range(2)]
                at = per_slot.get(slot, ())
                for g in at:
                    if g >= len(groups):
                        continue
                    j, half = groups[g]
                    if g == 0:
                        pe.wait_ge(wsum_ready, B + 1)
                    last = weighted(E[bset], wsum[bset], j, half, opens and j == 0, closes and j == tiles - 1)
                    if g == len(groups) - 1:
                        last.then_inc(r_batch_done, 1)

            EARLY = {5: (0, 1), 6: (2, 3), 7: (4, 5)}
            SPREAD = {5: (0,), 6: (1,), 7: (2,), 8: (3,), 9: (4, 5)}

            pe.wait_ge(c_silu, 1)
            for b in range(NB):
                for n in range(3):
                    at = 3 * b + n
                    for k in range(2):
                        last = pe.matmul(S[at // 2][:, at % 2, :], cwide[:, k, b, :], wmod_s[:, k, n * 512:(n + 1) * 512],
                                         start=(k == 0), stop=(k == 1))
            last.then_inc(mod_ready, 1)
            pe.wait_ge(consts_ready, 1)
            for kind in PRE_PIECES:
                pre_piece(-1, kind)
            pe.wait_ge(rows_ready, 1)

            PRE_AT = {(1, 3): "h1T", (1, 5): "Q", (1, 7): "K", (2, 3): "V"}
            POST_AT = {(1, 1): "Wo", (1, 10): "h2T", (2, 1): "logits", (2, 6): "gT", (2, 9): "b2"}

            def pe_block(i, parity, pre, att, post):
                if att:
                    pe.wait_ge(qk_in, 16 * 2 * len(TERMS) * (i + 1))
                for b, (first, tiles) in enumerate(HEAD):
                    B = batch_index(i, b)
                    prev = 3 if b == 0 else HEAD[b - 1][1]
                    for slot in range(NCHUNK * tiles):
                        if att:
                            scores(i, first, slot, parity)
                        if (b == 0 and post) or (b > 0 and att):
                            if b == 1 and slot == 5:
                                pe.wait_ge(r_taken, i)
                            weighted_batch(B - 1, prev, set_of(parity, b - 1), b == 1, b == 0, EARLY if b == 0 else SPREAD, slot)
                        if post and (b, slot) in POST_AT:
                            post_piece(i, POST_AT[b, slot], parity)
                        if pre and (b, slot) in PRE_AT:
                            pre_piece(i, PRE_AT[b, slot])
                with pe.Fori(0, BODY_ITERS) as it:
                    for h in range(2):
                        b = len(HEAD) + 2 * it + h
                        first = BODY_FIRST + 6 * it + 3 * h
                        for slot in range(NCHUNK * 3):
                            if att:
                                scores(i, first, slot, parity)
                                weighted_batch(batch_index(i, b) - 1, 3, set_of(parity, len(HEAD) + h - 1), False, False, SPREAD, slot)
                            if post and slot in EXPERT_AT:
                                expert_piece(i, EXPERT_AT[slot], 2 * it + h)

            EXPERT_AT = {1: "F01", 4: "F23", 11: "Y"}
            over_blocks(pe, pe_block)


        @block.scalar
        def _(act):
            def exp_chunk(i, first, slot, b, bset):
                j, ch = slot // NCHUNK, slot % NCHUNK
                if slot == 0:
                    if due(batch_index(i, b) - 1):
                        act.wait_ge(r_batch_done, batch_index(i, b) - 1)
                act.wait_ge(max_ready, SLOTS * i + NCHUNK * first + slot + 1)
                nc.scalar.activation(E[bset][j][:, ch * CHUNK:(ch + 1) * CHUNK].rearrange("p (h n) -> p h n", h=2),
                                     S[score_buffer(first, slot)][:, :, :], ACT.Exp, bias=nmax[bset][:, j, ch:ch + 1],
                                     accum_out=zc[bset][:, j, ch:ch + 1]).then_inc(exp_done, 1)

            def exp_maxima(i, b, tiles, bset):
                act.wait_ge(dmax_ready, batch_index(i, b) + 1)
                nc.scalar.activation(emax[bset][:, 0:tiles, :], dmax[bset][:, 0:tiles, :], ACT.Exp).then_inc(emax_ready, 1)

            def pre_take(i, kind, parity):
                act.wait_ge(m_ready, piece_no(i, kind) + 1)
                if kind == "h1T":
                    last = nc.scalar.activation(h1T[:, :, :], M[:, :, :], ACT.Copy)
                else:
                    if kind != "V":
                        act.wait_ge(q_split if kind == "Q" else k_split, i + 1)
                    dst, bias, scale = {"Q": (qf, bq_c, 1.0 / D), "K": (kf, bk_c, 1.0), "V": (vT[parity], bv_c, 1.0)}[kind]
                    for m in range(2):
                        last = nc.scalar.activation(dst[:, m, :], M[:, m, :], ACT.Identity, bias=bias[:, m:m + 1], scale=scale)
                last.then_inc(m_taken, 1)

            def post_take(i, kind):
                if kind == "gate exp":
                    act.wait_ge(lgd_ready, i)
                    nc.scalar.activation(lge[:, :, :], lgd[:, :, :], ACT.Exp).then_inc(lge_ready, 1)
                    return
                act.wait_ge(m_ready, piece_no(i, kind) + 1)
                if kind == "h2T":
                    nc.scalar.activation(h2T[:, :, :], M[:, :, :], ACT.Copy).then_inc(m_taken, 1)
                else:
                    nc.scalar.activation(gT[:, :], M[0:NE, 0, :], ACT.Copy).then_inc(m_taken, 1)

            def hidden_take(i, kind, e):
                act.wait_ge(m_ready, piece_no(i, kind, e) + 1)
                for n in range(2):
                    f = (0 if kind == "F01" else 2) + n
                    last = nc.scalar.activation(hid[:, f, :], M[:, n, :], ACT.Relu, bias=b1_c[:, e, f:f + 1])
                last.then_inc(m_taken, 1)

            act.wait_ge(consts_in, 16 * CONST_LOADS)
            nc.scalar.activation(csig, cT, ACT.Exp, scale=-1.0).then_inc(c_exp, 1)
            act.wait_ge(rows_ready, 1)
            for kind in PRE_PIECES:
                pre_take(-1, kind, 0)

            PRE_AT = {(1, 2): "h1T", (1, 4): "Q", (1, 6): "K", (2, 3): "V"}
            POST_AT = {(1, 9): "h2T", (2, 2): "gate exp", (2, 6): "gT"}
            EXPERT_AT = {1: "F01", 4: "F23"}

            def act_block(i, parity, pre, att, post):
                for b, (first, tiles) in enumerate(HEAD):
                    for slot in range(NCHUNK * tiles):
                        if att:
                            exp_chunk(i, first, slot, b, set_of(parity, b))
                        if post and (b, slot) in POST_AT:
                            post_take(i, POST_AT[b, slot])
                        if pre and (b, slot) in PRE_AT:
                            pre_take(i, PRE_AT[b, slot], 1 - parity)
                    if att:
                        exp_maxima(i, b, tiles, set_of(parity, b))
                with act.Fori(0, BODY_ITERS) as it:
                    for h in range(2):
                        b = len(HEAD) + 2 * it + h
                        bset = set_of(parity, len(HEAD) + h)
                        for slot in range(NCHUNK * 3):
                            if att:
                                exp_chunk(i, BODY_FIRST + 6 * it + 3 * h, slot, b, bset)
                            if post and slot in EXPERT_AT:
                                hidden_take(i, EXPERT_AT[slot], 2 * it + h)
                        if att:
                            exp_maxima(i, b, 3, bset)

            over_blocks(act, act_block)

        @block.vector
        def _(dve):
            def chunk_max(i, first, slot, bset):
                n = SLOTS * i + NCHUNK * first + slot + 1
                dve.wait_ge(scores_ready, n)
                dve.tensor_reduce(nmax[bset][:, slot // NCHUNK, slot % NCHUNK:slot % NCHUNK + 1],
                                  S[score_buffer(first, slot)][:, :, :], AX.XY, ALU.max, negate=True).then_inc(max_ready, 1)
                return n

            def all_max(done, tiles, bset):
                dve.wait_ge(max_ready, done)
                dve.tensor_reduce(nall[bset][:, 0:tiles], nmax[bset][:, 0:tiles, :], AX.X, ALU.min).then_inc(nall_ready, 1)

            def denominators(B, tiles, bset):
                dve.wait_ge(zz_ready, B + 1)
                dve.tensor_reduce(zsum[bset][:, 0:tiles], zz[bset][:, 0:tiles, :], AX.X, ALU.add).then_inc(zsum_ready, 1)
                dve.wait_ge(zsum_ready, B + 1)
                dve.reciprocal(rz[bset][:, 0:tiles], zsum[bset][:, 0:tiles]).then_inc(rz_ready, 1)

            def layer_stats(name, src, n):
                st, mv, _, _ = ln[name]
                bn_done, mean_ready = stats[name][0:2]
                for t in range(2):
                    dve.bn_stats(st[:, t, :], src[:, t, :]).then_inc(bn_done, 1)
                dve.wait_ge(bn_done, 2 * (n + 1))
                on_its_own(dve, 2 * (n + 1))
                for t in range(2):
                    dve.bn_aggr(mv[:, t, :], st[:, t, :]).then_inc(mean_ready, 1)

            def normalise(name, dst, src, n):
                _, mv, _, rs = ln[name]
                dve.wait_ge(stats[name][1], 2 * (n + 1))
                dve.wait_ge(stats[name][3], n + 1)
                for t in range(2):
                    dve.tensor_scalar(dst[:, t, :], src[:, t, :], mv[:, t, 0:1], rs[:, t:t + 1],
                                      ALU.subtract, ALU.mult).then_inc(stats[name][4], 1)

            def residual(i, parity):
                at = piece_no(i, "Wo") + 1
                dve.wait_ge(m_ready, at)
                dve.tensor_tensor(ao[:, :, :], M[:, :, :], rows_of_batch(ga_r, i - 1), ALU.mult).then_inc(m_taken, 1)
                dve.wait_ge(m_taken, at)
                dve.wait_ge(x1_biased, i)
                dve.tensor_tensor(x1[1 - parity][:, :, :], x1[1 - parity][:, :, :], ao[:, :, :], ALU.add).then_inc(x1_ready, 1)
                dve.wait_ge(x1_ready, i)
                layer_stats("two", x1[1 - parity], i - 1)

            def logits(i):
                at = piece_no(i, "logits") + 1
                dve.wait_ge(m_ready, at)
                dve.tensor_tensor(lg[:, :, :], M[:, :, 0:NE], bg_r[:, :].unsqueeze(1).to_broadcast([P, 2, NE]), ALU.add).then_inc(m_taken, 1)
                dve.wait_ge(m_taken, at)
                link = Chain(dve, gate_link, GATE_LINKS * (i - 1))
                link(dve.tensor_reduce(top[:, :], lg[:, :, :], AX.X, ALU.max))
                dve.tensor_tensor(lgd[:, :, :], lg[:, :, :], top[:, :].unsqueeze(2).to_broadcast([P, 2, NE]),
                                  ALU.subtract).then_inc(lgd_ready, 1)

            def routing(i):
                link = Chain(dve, gate_link, GATE_LINKS * (i - 1) + 1)
                other = lg[:, :, :].unsqueeze(2).to_broadcast([P, 2, NE, NE])
                own = lg[:, :, :].unsqueeze(3).to_broadcast([P, 2, NE, NE])
                before = earlier[:, :, :].unsqueeze(1).to_broadcast([P, 2, NE, NE])
                dve.tensor_tensor(gt[:, :, :, :], other, own, ALU.is_gt)
                link(dve.tensor_tensor(eq[:, :, :, :], other, own, ALU.is_equal))
                link(dve.tensor_tensor(eq[:, :, :, :], eq[:, :, :, :], before, ALU.mult))
                link(dve.tensor_tensor(gt[:, :, :, :], gt[:, :, :, :], eq[:, :, :, :], ALU.add))
                link(dve.tensor_reduce(rank[:, :, :], gt[:, :, :, :], AX.X, ALU.add))
                dve.wait_ge(lge_ready, i)
                link(dve.scalar_tensor_tensor(chosen[:, :, :], rank[:, :, :], 1.5, lge[:, :, :], ALU.is_lt, ALU.mult))
                link(dve.tensor_reduce(gsum[:, :], chosen[:, :, :], AX.X, ALU.add))
                link(dve.reciprocal(grec[:, :], gsum[:, :]))
                dve.tensor_tensor(gate[:, :, :], chosen[:, :, :], grec[:, :].unsqueeze(2).to_broadcast([P, 2, NE]),
                                  ALU.mult).then_inc(gate_ready, 1)

            def start_y(i):
                dve.wait_ge(m_ready, piece_no(i, "b2") + 1)
                dve.tensor_tensor(y[:, :, :], M[:, :, :], h2[:, :, :], ALU.add).then_inc(m_taken, 1)

            def add_expert(i, e):
                at = piece_no(i, "Y", e) + 1
                dve.wait_ge(m_taken, at - 3 if not isinstance(e, int) else at - 1)
                dve.wait_ge(m_ready, at)
                for t in range(2):
                    last = dve.scalar_tensor_tensor(y[:, t, :], M[:, t, :], gate[:, t, bass.ds(e, 1)], y[:, t, :], ALU.mult, ALU.add)
                last.then_inc(m_taken, 1)

            link = Chain(dve, c_link, 0)
            dve.wait_ge(c_exp, 1)
            link(dve.tensor_scalar(csig, csig, 1.0, None, ALU.add))
            link(dve.reciprocal(csil, csig))
            link(dve.tensor_tensor(csil, csil, cT, ALU.mult))
            for k in range(2):
                for b in range(NB):
                    last = dve.tensor_copy(cwide[:, k, b, :], csil[:, k, b:b + 1].to_broadcast([P, P]))
            last.then_inc(c_silu, 1)
            dve.wait_ge(x_in, 16)
            layer_stats("one", xin, 0)
            normalise("one", xin, xin, 0)
            dve.wait_ge(mod_ready, 1)
            link = Chain(dve, mod_link, 0)
            for b in range(NB):
                for n in range(3):
                    at = 3 * b + n
                    last = dve.tensor_copy(modr[b][:, n * 512:(n + 1) * 512], S[at // 2][:, at % 2, :])
            link(last)
            for b in range(NB):
                part = [modr[b][:, n * D:(n + 1) * D] for n in range(6)]
                dve.tensor_copy(sa_r[:, b, :], part[0])
                dve.tensor_scalar(c1a_r[:, b, :], part[1], 1.0, None, ALU.add)
                dve.tensor_copy(sb_r[:, b, :], part[3])
                dve.tensor_scalar(c1b_r[:, b, :], part[4], 1.0, None, ALU.add)
                for g, at in ((part[2], 0), (part[5], 1)):
                    link(dve.tensor_scalar(scr[:, at, :], g, -1.0, None, ALU.mult))
                    link(dve.tensor_tensor(scr[:, at, :], scr[:, at, :], g, ALU.max))
                    link(dve.tensor_scalar(scr[:, at, :], scr[:, at, :], 0.25, None, ALU.max))
                    link(dve.tensor_scalar(scr2[:, at, :], g, 0.0, 2.0, ALU.is_ge, ALU.mult))
                    link(dve.tensor_scalar(scr2[:, at, :], scr2[:, at, :], -1.0, None, ALU.add))
                    link(dve.tensor_tensor(scr3[:, at, :], scr[:, at, :], scr2[:, at, :], ALU.mult))
                dve.tensor_copy(ga_r[:, b, :], scr3[:, 0, :])
                dve.tensor_tensor(gabo_r[:, b, :], scr3[:, 0, :], bo_r, ALU.mult)
                dve.tensor_tensor(gscale_r[:, b, :], scr3[:, 1, :], gamma_r, ALU.mult)
                link(dve.tensor_tensor(gshift_r[:, b, :], scr3[:, 1, :], beta_r, ALU.mult))
            dve.tensor_scalar(bq_c[:, :], bq_c[:, :], 1.0 / D, None, ALU.mult).then_inc(rows_ready, 1)
            dve.wait_ge(rows_ready, 1)

            def dve_block(i, parity, pre, att, post):
                for b, (first, tiles) in enumerate(HEAD):
                    prev = 3 if b == 0 else HEAD[b - 1][1]
                    done = 0
                    for slot in range(NCHUNK * tiles):
                        if att:
                            done = chunk_max(i, first, slot, set_of(parity, b))
                        if slot == 2 and ((b == 0 and post) or (b > 0 and att)):
                            denominators(batch_index(i, b) - 1, prev, set_of(parity, b - 1))
                        if pre and (b, slot) == (0, 1):
                            dve.wait_ge(x_in, 16 * (i + 2))
                            layer_stats("one", xin, i + 1)
                        if pre and (b, slot) == (0, 3):
                            normalise("one", xin, xin, i + 1)
                        if post and (b, slot) == (0, 7):
                            dve.wait_ge(r_batch_done, batch_index(i, 0))
                            dve.tensor_tensor(vT[1 - parity][:, :, :], R[:, :, :], vT[1 - parity][:, :, :], ALU.mult).then_inc(r_taken, 1)
                        if post and (b, slot) == (1, 1):
                            residual(i, parity)
                        if post and (b, slot) == (1, 4):
                            normalise("two", h2, x1[1 - parity], i - 1)
                        if post and (b, slot) == (2, 1):
                            logits(i)
                        if post and (b, slot) == (2, 4):
                            routing(i)
                        if post and (b, slot) == (2, 9):
                            start_y(i)
                    if att:
                        all_max(done, tiles, set_of(parity, b))
                with dve.Fori(0, BODY_ITERS) as it:
                    for h in range(2):
                        b = len(HEAD) + 2 * it + h
                        bset = set_of(parity, len(HEAD) + h)
                        done = 0
                        for slot in range(NCHUNK * 3):
                            if att:
                                done = chunk_max(i, BODY_FIRST + 6 * it + 3 * h, slot, bset)
                            if att and slot == 2:
                                denominators(batch_index(i, b) - 1, 3, 1 - bset)
                        if att:
                            all_max(done, 3, bset)
                        if post:
                            add_expert(i, 2 * it + h)
                if post:
                    dve.wait_ge(m_taken, piece_no(i, "Y", NE - 1) + 1)
                    layer_stats("out", y, i - 1)
                    normalise("out", y, y, i - 1)

            over_blocks(dve, dve_block)

        @block.gpsimd
        def _(pool):
            def max_differences(i, b, tiles, bset):
                pool.wait_ge(nall_ready, batch_index(i, b) + 1)
                pool.tensor_tensor(dmax[bset][:, 0:tiles, :], nall[bset][:, 0:tiles].unsqueeze(2).to_broadcast([P, tiles, NCHUNK]),
                                   nmax[bset][:, 0:tiles, :], ALU.subtract).then_inc(dmax_ready, 1)

            def chunk_sums(B, tiles, bset):
                pool.wait_ge(emax_ready, B + 1)
                pool.tensor_tensor(zz[bset][:, 0:tiles, :], zc[bset][:, 0:tiles, :], emax[bset][:, 0:tiles, :], ALU.mult).then_inc(zz_ready, 1)

            def weights(B, tiles, bset):
                pool.wait_ge(rz_ready, B + 1)
                pool.tensor_tensor(wc[bset][:, 0:tiles, :], emax[bset][:, 0:tiles, :],
                                   rz[bset][:, 0:tiles].unsqueeze(2).to_broadcast([P, tiles, NCHUNK]), ALU.mult).then_inc(wc_ready, 1)
                pool.wait_ge(wc_ready, B + 1)
                if due(B - 1):
                    pool.wait_ge(r_batch_done, B - 1)
                    on_its_own(pool, B - 1)
                for e in range(2):
                    last = pool.tensor_copy(wsum[bset][:, 0:tiles, :, e, DH * e:DH * (e + 1)],
                                            wc[bset][:, 0:tiles, :].unsqueeze(3).to_broadcast([P, tiles, NCHUNK, DH]))
                last.then_inc(wsum_ready, 1)

            def inverse_deviation(name, n):
                _, mv, ve, rs = ln[name]
                _, mean_ready, ve_ready, rstd_ready, _ = stats[name]
                pool.wait_ge(mean_ready, 2 * (n + 1))
                on_its_own(pool, 2 * (n + 1))
                pool.tensor_scalar(ve[:, :], mv[:, :, 1], EPS, None, ALU.add).then_inc(ve_ready, 1)
                pool.wait_ge(ve_ready, n + 1)
                pool.tensor_tensor(rs[:, :], ve[:, :], mhalf[:, :], ALU.pow).then_inc(rstd_ready, 1)

            def modulate(name, buf, scale_r, shift_r, n, linked, ready):
                pool.wait_ge(stats[name][4], 2 * (n + 1))
                pool.tensor_tensor(buf[:, :, :], buf[:, :, :], rows_of_batch(scale_r, n), ALU.mult).then_inc(linked, 1)
                pool.wait_ge(linked, n + 1)
                pool.tensor_tensor(buf[:, :, :], buf[:, :, :], rows_of_batch(shift_r, n), ALU.add).then_inc(ready, 1)

            def split(i, kind, src, parts, linked, done):
                pool.wait_ge(m_taken, piece_no(i, kind) + 1)
                if due(16 * (i + 1)):
                    pool.wait_ge(q_parts_out if kind == "Q" else k_parts_out, 16 * (i + 1))
                    on_its_own(pool, 16 * (i + 1))
                link = Chain(pool, linked, SPLIT_LINKS * (i + 1))
                link(pool.tensor_copy(parts[:, HI, :, :], src[:, :, :]))
                link(pool.tensor_tensor(src[:, :, :], src[:, :, :], parts[:, HI, :, :], ALU.subtract))
                link(pool.tensor_copy(parts[:, MID, :, :], src[:, :, :]))
                pool.tensor_tensor(parts[:, LO, :, :], src[:, :, :], parts[:, MID, :, :], ALU.subtract).then_inc(done, 1)

            def bias_residual(i, parity):
                pool.wait_ge(x1_in, 16 * i)
                pool.tensor_tensor(x1[1 - parity][:, :, :], x1[1 - parity][:, :, :], rows_of_batch(gabo_r, i - 1), ALU.add).then_inc(x1_biased, 1)

            def finish(i, parity):
                inverse_deviation("out", i - 1)
                pool.wait_ge(stats["out"][4], 2 * i)
                link = Chain(pool, out_link, 2 * (i - 1))
                link(pool.tensor_tensor(y[:, :, :], y[:, :, :], rows_of_batch(gscale_r, i - 1), ALU.mult))
                link(pool.tensor_tensor(y[:, :, :], y[:, :, :], rows_of_batch(gshift_r, i - 1), ALU.add))
                pool.tensor_tensor(y[:, :, :], y[:, :, :], x1[1 - parity][:, :, :], ALU.add).then_inc(out_ready, 1)

            pool.memset(mhalf[:, :], -0.5)
            pool.memset(wsum[0][:, :, :, :, :], 0.0)
            pool.memset(wsum[1][:, :, :, :, :], 0.0)
            pool.memset(earlier[:, :, :], 1.0)
            pool.memset(ident[:, :], 0.0).then_inc(ident_zeroed, 1)
            pool.wait_ge(ident_zeroed, 1)
            pool.affine_select(out=earlier[:, :, :], in_=earlier[:, :, :], compare_op=ALU.is_gt, fill=0.0, base=0,
                               pattern=[[1, NE], [-1, NE]], channel_multiplier=0)
            pool.affine_select(out=ident[:, :], in_=ident[:, :], compare_op=ALU.not_equal, fill=1.0, base=0,
                               pattern=[[-1, P]], channel_multiplier=1).then_inc(consts_ready, 1)
            pool.wait_ge(consts_ready, 1)
            inverse_deviation("one", 0)
            pool.wait_ge(rows_ready, 1)
            modulate("one", xin, c1a_r, sa_r, 0, h1_link, h1_ready)
            split(-1, "Q", qf, qparts, q_link, q_split)
            split(-1, "K", kf, kparts, k_link, k_split)

            def pool_block(i, parity, pre, att, post):
                for b, (first, tiles) in enumerate(HEAD):
                    prev = 3 if b == 0 else HEAD[b - 1][1]
                    B = batch_index(i, b)
                    if b == 0 and pre:
                        inverse_deviation("one", i + 1)
                    if (b == 0 and post) or (b > 0 and att):
                        chunk_sums(B - 1, prev, set_of(parity, b - 1))
                    if b == 1 and post:
                        inverse_deviation("two", i - 1)
                    if (b == 0 and post) or (b > 0 and att):
                        weights(B - 1, prev, set_of(parity, b - 1))
                    if b == 0 and post:
                        bias_residual(i, parity)
                    if b == 1 and post:
                        modulate("two", h2, c1b_r, sb_r, i - 1, h2_link, h2_ready)
                    if att:
                        max_differences(i, b, tiles, set_of(parity, b))
                    if b == 0 and pre:
                        modulate("one", xin, c1a_r, sa_r, i + 1, h1_link, h1_ready)
                    if b == 1 and pre:
                        split(i, "Q", qf, qparts, q_link, q_split)
                if pre:
                    split(i, "K", kf, kparts, k_link, k_split)
                if att:
                    with pool.Fori(0, BODY_ITERS) as it:
                        for h in range(2):
                            b = len(HEAD) + 2 * it + h
                            bset = set_of(parity, len(HEAD) + h)
                            chunk_sums(batch_index(i, b) - 1, 3, 1 - bset)
                            weights(batch_index(i, b) - 1, 3, 1 - bset)
                            max_differences(i, b, 3, bset)
                if post:
                    finish(i, parity)

            over_blocks(pool, pool_block)


_INS = ['L0_attn_X_embed', 'L0_attn_Wq', 'L0_attn_bq', 'L0_attn_Wk', 'L0_attn_bk', 'L0_attn_Wv', 'L0_attn_bv', 'L0_attn_Wo', 'L0_attn_bo', 'L0_ffn_Wg', 'L0_ffn_bg', 'L0_ffn_W1', 'L0_ffn_b1', 'L0_ffn_W2', 'L0_ffn_b2', 'L0_ffn_gamma', 'L0_ffn_beta', 'L0_c', 'L0_wmod']
_OUT = ((2, 4096, 256), "float32")


def kernel(**inputs):
    import numpy as _np
    import concourse.bacc as _bacc
    from concourse import mybir as _mybir
    from concourse.bass_utils import run_bass_kernel_spmd as _run

    nc = _bacc.Bacc("TRN2", target_bir_lowering=False, num_devices=1)
    arrays, args = {}, []
    for name in _INS:
        a = _np.ascontiguousarray(inputs[name])
        arrays[f"in_{name}"] = a
        args.append(nc.dram_tensor(f"in_{name}", a.shape, _mybir.dt.from_np(a.dtype), kind="ExternalInput").ap())
    out = nc.dram_tensor("out", _OUT[0], _mybir.dt.from_np(_np.dtype(_OUT[1])), kind="ExternalOutput").ap()
    adaln_layer(nc, *args, out)
    r = _run(nc, [arrays], core_ids=[0])
    return r.results[0]["out"]
```

```python
from contextlib import ExitStack

import concourse.bass as bass
from concourse import mybir

F32 = mybir.dt.float32
BF16 = mybir.dt.bfloat16
ALU = mybir.AluOpType
ACT = mybir.ActivationFunctionType
AX = mybir.AxisListType

P = 128
ROWS = 256
D = 256
DH = 16
GROUPS = D // DH
POS = ROWS * GROUPS
CHUNK = 1024
NCHUNK = POS // CHUNK
TILES = POS // P
NE = 8
FF = 512
NF = FF // P
NB = 2
BLOCKS = NB * 4096 // ROWS
EPS = 1e-5
SLOTS = NCHUNK * TILES
QUARTER = POS // 4

HEAD = ((0, 2), (2, 3), (5, 3))
BODY_FIRST = 8
BODY_ITERS = 4
BATCHES = len(HEAD) + 2 * BODY_ITERS
POOL_STEPS = 3 + 3 * 2 * BODY_ITERS

HI, MID, LO = range(3)
TERMS = ((HI, HI), (HI, MID), (MID, HI), (HI, LO), (LO, HI), (MID, MID), (MID, LO), (LO, MID))

PRE_PIECES = ("h1T", "Q", "K", "V")
HEAD_PIECES = ("h1T", "Wo", "Q", "K", "h2T", "logits", "V", "gT", "b2")
POST_PIECES = tuple(k for k in HEAD_PIECES if k not in PRE_PIECES)
EXPERT_PIECES = ("F01", "F23", "Y")
PER_BLOCK = len(HEAD_PIECES) + NE * len(EXPERT_PIECES)


GATE_LINKS = 8
CONST_LOADS = 19


def piece_no(i, kind, e=0):
    fixed = isinstance(i, int)
    if fixed and i < 1:
        return len(PRE_PIECES) * (i + 1) + PRE_PIECES.index(kind)
    base = 2 * len(PRE_PIECES) + PER_BLOCK * (i - 1)
    kinds = HEAD_PIECES
    if fixed and i >= BLOCKS - 1:
        kinds = POST_PIECES
        base = base - (len(PRE_PIECES) if i >= BLOCKS else 0)
    if kind in EXPERT_PIECES:
        return base + len(kinds) + len(EXPERT_PIECES) * e + EXPERT_PIECES.index(kind)
    return base + kinds.index(kind)


def adaln_layer(nc, x, Wq, bq, Wk, bk, Wv, bv, Wo, bo, Wg, bg, W1, b1, W2, b2, gamma, beta, c, wmod, out):
    with ExitStack() as ctx:
        def sb(name, shape, dt=F32):
            return ctx.enter_context(nc.sbuf_tensor(name, shape, dt))

        def ps(name, shape):
            return ctx.enter_context(nc.psum_tensor(name, shape, F32))

        def sem(name):
            return ctx.enter_context(nc.semaphore(name))

        E = [[sb(f"E{s}{j}", [P, POS]) for j in range(3)] for s in range(2)]
        qT = [sb(f"qT{s}", [P, POS], BF16) for s in range(2)]
        kT = [sb(f"kT{s}", [P, POS], BF16) for s in range(2)]
        wsum = [sb(f"wsum{s}", [P, 3, NCHUNK, 3 * DH]) for s in range(2)]
        pool_sum = sb("pool_sum", [P, QUARTER])
        ones_col = sb("ones_col", [P, 32])
        xin = sb("xin", [P, 2, D])
        h1T = sb("h1T", [P, 2, ROWS])
        qf = sb("qf", [P, 2, ROWS])
        kf = sb("kf", [P, 2, ROWS])
        qparts = sb("qparts", [P, 3, 2, ROWS], BF16)
        kparts = sb("kparts", [P, 3, 2, ROWS], BF16)
        vT = [sb(f"vT{s}", [P, 2, ROWS]) for s in range(2)]
        x1 = [sb(f"x1{s}", [P, 2, D]) for s in range(2)]
        h2 = sb("h2", [P, 2, D])
        h2T = sb("h2T", [P, 2, ROWS])
        y = sb("y", [P, 2, D])
        w1s = sb("w1s", [P, 2, FF])
        w2s = sb("w2s", [P, NF, D])
        hid = sb("hid", [P, NF, ROWS])
        wq_s, wk_s, wv_s, wo_s = (sb(n, [P, 2, D]) for n in ("wq_s", "wk_s", "wv_s", "wo_s"))
        wg_s = sb("wg_s", [P, 2, NE])
        b2_s = sb("b2_s", [NE, D])
        ident = sb("ident", [P, P])
        earlier = sb("earlier", [P, NE, NE])
        mod_names = ("sa", "c1a", "ga", "sb", "c1b", "gb")
        sa_r, c1a_r, ga_r, sb_r, c1b_r, gscale_r = (sb(f"{n}_r", [P, NB, D]) for n in mod_names)
        gabo_r = sb("gabo_r", [P, NB, D])
        gshift_r = sb("gshift_r", [P, NB, D])
        bg_r = sb("bg_r", [P, NE])
        bq_c, bk_c, bv_c = (sb(n, [P, 2]) for n in ("bq_c", "bk_c", "bv_c"))
        b1_c = sb("b1_c", [P, NE, NF])
        nmax = [sb(f"nmax{s}", [P, 3, NCHUNK]) for s in range(2)]
        zc = [sb(f"zc{s}", [P, 3, NCHUNK]) for s in range(2)]
        nall = [sb(f"nall{s}", [P, 3]) for s in range(2)]
        dmax = [sb(f"dmax{s}", [P, 3, NCHUNK]) for s in range(2)]
        emax = [sb(f"emax{s}", [P, 3, NCHUNK]) for s in range(2)]
        zz = [sb(f"zz{s}", [P, 3, NCHUNK]) for s in range(2)]
        zsum = [sb(f"zsum{s}", [P, 3]) for s in range(2)]
        rz = [sb(f"rz{s}", [P, 3]) for s in range(2)]
        ln = {n: (sb(f"st_{n}", [P, 2, 6]), sb(f"mv_{n}", [P, 2, 2]), sb(f"ve_{n}", [P, 2]), sb(f"rs_{n}", [P, 2]))
              for n in ("one", "two", "out")}
        mhalf = sb("mhalf", [P, 2])
        lg = sb("lg", [P, 2, NE])
        top = sb("top", [P, 2])
        lgd = sb("lgd", [P, 2, NE])
        lge = sb("lge", [P, 2, NE])
        gt = sb("gt", [P, 2, NE, NE])
        eq = sb("eq", [P, 2, NE, NE])
        rank = sb("rank", [P, 2, NE])
        chosen = sb("chosen", [P, 2, NE])
        gsum = sb("gsum", [P, 2])
        grec = sb("grec", [P, 2])
        gate = sb("gate", [P, 2, NE])
        gT = sb("gT", [NE, ROWS])

        S = [ps(f"S{n}", [P, 2, 512]) for n in range(3)]
        R = ps("R", [P, 2, ROWS])
        M = ps("M", [P, 2, ROWS])

        q_dram = nc.dram_tensor("q_dram", [3, GROUPS, DH, ROWS], BF16, kind="Internal").ap()
        k_dram = nc.dram_tensor("k_dram", [3, GROUPS, DH, ROWS], BF16, kind="Internal").ap()

        wmod_s = E[0][0][:, 0:2 * 1536].rearrange("p (k n) -> p k n", k=2)
        cT = E[0][1][:, 0:4].rearrange("p (k b) -> p k b", k=2)
        csig = E[0][1][:, 8:12].rearrange("p (k b) -> p k b", k=2)
        csil = E[0][1][:, 16:20].rearrange("p (k b) -> p k b", k=2)
        cwide = E[0][1][:, 1024:1024 + 4 * P].rearrange("p (k b m) -> p k b m", k=2, b=2)
        modr = [E[0][2][:, 0:1536], E[0][2][:, 1536:3072]]
        bo_r = E[1][0][:, 0:D]
        gamma_r = E[1][0][:, D:2 * D]
        beta_r = E[1][0][:, 2 * D:3 * D]
        scr = E[1][1][:, 0:2 * D].rearrange("p (b d) -> p b d", b=2)
        scr2 = E[1][1][:, 2 * D:4 * D].rearrange("p (b d) -> p b d", b=2)
        scr3 = E[1][1][:, 4 * D:6 * D].rearrange("p (b d) -> p b d", b=2)

        waits_passed = sem("waits_passed")
        consts_in = sem("consts_in")
        x_in, x1_in, w1_in, w2_in = sem("x_in"), sem("x1_in"), sem("w1_in"), sem("w2_in")
        q_parts_out, k_parts_out, qk_in, stored = sem("q_parts_out"), sem("k_parts_out"), sem("qk_in"), sem("stored")
        consts_ready = sem("consts_ready")
        ident_zeroed = sem("ident_zeroed")
        c_exp, c_silu, c_link = sem("c_exp"), sem("c_silu"), sem("c_link")
        mod_ready, mod_taken, mod_link, rows_ready = sem("mod_ready"), sem("mod_taken"), sem("mod_link"), sem("rows_ready")
        scores_ready, max_ready, exp_done = sem("scores_ready"), sem("max_ready"), sem("exp_done")
        nall_ready, dmax_ready, emax_ready, zz_ready = sem("nall_ready"), sem("dmax_ready"), sem("emax_ready"), sem("zz_ready")
        zsum_ready, rz_ready, wsum_ready = sem("zsum_ready"), sem("rz_ready"), sem("wsum_ready")
        r_tile_done, r_taken = sem("r_tile_done"), sem("r_taken")
        pool_scaled, pool_steps, pool_sum_used = sem("pool_scaled"), sem("pool_steps"), sem("pool_sum_used")
        m_ready, m_taken = sem("m_ready"), sem("m_taken")
        stats = {n: (sem(f"bn_{n}"), sem(f"mean_ready_{n}"), sem(f"ve_ready_{n}"), sem(f"rstd_ready_{n}"),
                     sem(f"norm_ready_{n}")) for n in ("one", "two", "out")}
        h1_scaled, h1_ready, h2_scaled, h2_ready = sem("h1_scaled"), sem("h1_ready"), sem("h2_scaled"), sem("h2_ready")
        hi_ready, rest_ready, mid_ready, q_split, k_split = (sem(n) for n in ("hi_ready", "rest_ready", "mid_ready", "q_split", "k_split"))
        x1_biased, x1_ready, x1_shifted = sem("x1_biased"), sem("x1_ready"), sem("x1_shifted")
        gate_link, lgd_ready, lge_ready, gate_ready = sem("gate_link"), sem("lgd_ready"), sem("lge_ready"), sem("gate_ready")
        out_scaled, out_ready = sem("out_scaled"), sem("out_ready")

        def due(count):
            return not isinstance(count, int) or count > 0

        def on_its_own(eng, count):
            if not isinstance(count, int):
                eng.sem_inc(waits_passed, 1)

        class Chain:
            def __init__(self, eng, s, done):
                self.eng, self.sem, self.done = eng, s, done

            def __call__(self, ins):
                self.done = self.done + 1
                ins.then_inc(self.sem, 1)
                self.eng.wait_ge(self.sem, self.done)
                on_its_own(self.eng, self.done)

        def over_blocks(eng, block):
            block(0, 0, pre=True, att=True, post=False)
            with eng.Fori(0, (BLOCKS - 2) // 2) as pair:
                block(2 * pair + 1, 1, pre=True, att=True, post=True)
                block(2 * pair + 2, 0, pre=True, att=True, post=True)
            block(BLOCKS - 1, 1, pre=False, att=True, post=True)
            block(BLOCKS, 0, pre=False, att=False, post=True)

        def batch_index(i, b):
            return BATCHES * i + b

        def set_of(parity, b):
            return (parity + b) % 2

        def score_buffer(first, slot):
            at = NCHUNK * (first if isinstance(first, int) else BODY_FIRST) + slot
            return at % 3

        def tile_cols(tile):
            return bass.ts(tile, P)

        x_blocks = x.rearrange("b (n t p) d -> (b n) p t d", t=2, p=P)
        out_blocks = out.rearrange("b (n t p) d -> (b n) p t d", t=2, p=P)

        def rows_of_batch(rows, i):
            return rows[:, i // (BLOCKS // NB), :].unsqueeze(1).to_broadcast([P, 2, D])

        def row_of_batch(rows, i):
            return rows[:, i // (BLOCKS // NB), :]

        block = ctx.enter_context(nc.Block())

        @block.sync
        def _(sp):
            loads = [0]

            def cload(dst, src):
                loads[0] += 1
                sp.dma_start(dst, src, allow_slow_non_contiguous=True).then_inc(consts_in, 16)

            sp.dma_start(xin[:, :, :], x_blocks[0]).then_inc(x_in, 16)
            cload(wmod_s, wmod.rearrange("(k p) n -> p k n", p=P))
            for b in range(NB):
                for k in range(2):
                    cload(cT[:, k, b:b + 1], c[b:b + 1, k * P:(k + 1) * P].rearrange("b p -> p b"))
            for dst, src in ((wq_s, Wq), (wk_s, Wk), (wv_s, Wv), (wo_s, Wo), (wg_s, Wg)):
                cload(dst[:, :, :], src.rearrange("(k p) n -> p k n", p=P))
            cload(b2_s[:, :], b2)
            for dst, src, n in ((bo_r, bo, D), (gamma_r, gamma, D), (beta_r, beta, D), (bg_r[:, :], bg, NE)):
                cload(dst, src.rearrange("(a n) -> a n", a=1).to_broadcast([P, n]))
            for dst, src in ((bq_c, bq), (bk_c, bk), (bv_c, bv)):
                cload(dst[:, :], src.rearrange("(k p) -> p k", p=P))
            cload(b1_c[:, :, :], b1.rearrange("e (f p) -> p e f", p=P))

            def load_expert_up(e):
                sp.dma_start(w1s[:, :, :], W1[e].rearrange("(k p) f -> p k f", p=P)).then_inc(w1_in, 16)

            def load_expert_down(e):
                sp.dma_start(w2s[:, :, :], W2[e].rearrange("(f p) n -> p f n", p=P)).then_inc(w2_in, 16)

            assert loads[0] == CONST_LOADS, loads
            load_expert_up(0)
            load_expert_down(0)

            def move_parts(n, parity):
                if due(n):
                    sp.wait_ge(qk_in, 16 * 2 * len(TERMS) * n)
                    on_its_own(sp, n)
                sp.wait_ge(q_split, n + 1)
                on_its_own(sp, n + 1)
                sp.dma_start(q_dram.rearrange("s (t g) d r -> (g d) s t r", t=2), qparts[:, :, :, :]).then_inc(q_parts_out, 16)
                sp.wait_ge(k_split, n + 1)
                on_its_own(sp, n + 1)
                sp.dma_start(k_dram.rearrange("s (t g) d r -> (g d) s t r", t=2), kparts[:, :, :, :]).then_inc(k_parts_out, 16)
                if due(SLOTS * (n - 1)):
                    sp.wait_ge(scores_ready, SLOTS * (n - 1))
                    on_its_own(sp, SLOTS * (n - 1))
                sp.wait_ge(q_parts_out, 16 * (n + 1))
                on_its_own(sp, 16 * (n + 1))
                sp.wait_ge(k_parts_out, 16 * (n + 1))
                on_its_own(sp, 16 * (n + 1))
                for t, (a, b) in enumerate(TERMS):
                    strip = slice(DH * t, DH * (t + 1))
                    for dst, src, part in ((qT, q_dram, a), (kT, k_dram, b)):
                        sp.dma_start(dst[parity][strip, :].rearrange("d (g r) -> d g r", g=GROUPS),
                                     src[part].rearrange("g d r -> d g r")).then_inc(qk_in, 16)

            def load_x(n):
                sp.dma_start(xin[:, :, :], x_blocks[n]).then_inc(x_in, 16)

            move_parts(0, 0)
            load_x(1)

            def sp_block(i, parity, pre, att, post):
                if post:
                    sp.dma_start(x1[1 - parity][:, :, :], x_blocks[i - 1]).then_inc(x1_in, 16)
                if pre:
                    move_parts(i + 1, 1 - parity)
                    load_x((i + 2) % BLOCKS)
                if post:
                    def refill(e_done, e_next):
                        sp.wait_ge(m_ready, piece_no(i, "F23", e_done) + 1)
                        on_its_own(sp, piece_no(i, "F23", e_done) + 1)
                        load_expert_up(e_next)
                        sp.wait_ge(m_ready, piece_no(i, "Y", e_done) + 1)
                        on_its_own(sp, piece_no(i, "Y", e_done) + 1)
                        load_expert_down(e_next)

                    with sp.Fori(0, BODY_ITERS - 1) as it:
                        refill(2 * it, 2 * it + 1)
                        refill(2 * it + 1, 2 * it + 2)
                    refill(NE - 2, NE - 1)
                    if att:
                        refill(NE - 1, 0)
                    sp.wait_ge(out_ready, i)
                    on_its_own(sp, i)
                    sp.dma_start(out_blocks[i - 1], y[:, :, :]).then_inc(stored, 16)
                    sp.wait_ge(stored, 16 * i)
                    on_its_own(sp, i)

            over_blocks(sp, sp_block)
            sp.wait_ge(q_parts_out, 16 * BLOCKS)
            sp.wait_ge(k_parts_out, 16 * BLOCKS)

        @block.tensor
        def _(pe):
            def bank_free(i, kind):
                if due(piece_no(i, kind)):
                    pe.wait_ge(m_taken, piece_no(i, kind))

            def transposes(dst, src):
                for k in range(2):
                    for t in range(2):
                        last = pe.transpose(dst[:, k, t * P:(t + 1) * P], src[:, t, k * P:(k + 1) * P], ident[:, :])
                return last

            def project(w, src, m):
                for k in range(2):
                    last = pe.matmul(M[:, m, :], w[:, k, m * P:(m + 1) * P], src[:, k, :], start=(k == 0), stop=(k == 1))
                return last

            def by_tokens(src, w, t, cols):
                for k in range(2):
                    last = pe.matmul(M[:, t, 0:cols], src[:, k, t * P:(t + 1) * P], w[:, k, :], start=(k == 0), stop=(k == 1))
                return last

            def pre_piece(i, kind, half):
                if half == 0:
                    bank_free(i, kind)
                if kind == "h1T":
                    pe.wait_ge(h1_ready, i + 2)
                    transposes(M, xin).then_inc(m_ready, 1)
                else:
                    if half == 0:
                        pe.wait_ge(m_taken, piece_no(i, "h1T") + 1)
                    last = project({"Q": wq_s, "K": wk_s, "V": wv_s}[kind], h1T, half)
                    if half == 1:
                        last.then_inc(m_ready, 1)

            def post_piece(i, kind, half, parity):
                if half == 0:
                    bank_free(i, kind)
                if kind == "Wo":
                    pe.wait_ge(r_taken, i)
                    last = by_tokens(vT[1 - parity], wo_s, half, D)
                    if half == 1:
                        last.then_inc(m_ready, 1)
                elif kind == "h2T":
                    pe.wait_ge(h2_ready, i)
                    transposes(M, h2).then_inc(m_ready, 1)
                elif kind == "logits":
                    pe.wait_ge(m_taken, piece_no(i, "h2T") + 1)
                    by_tokens(h2T, wg_s, 0, NE)
                    by_tokens(h2T, wg_s, 1, NE).then_inc(m_ready, 1)
                elif kind == "gT":
                    pe.wait_ge(gate_ready, i)
                    pe.transpose(M[0:NE, 0, 0:P], gate[:, 0, :], ident[:, :])
                    pe.transpose(M[0:NE, 0, P:2 * P], gate[:, 1, :], ident[:, :]).then_inc(m_ready, 1)
                elif kind == "b2":
                    pe.wait_ge(m_taken, piece_no(i, "gT") + 1)
                    pe.matmul(M[:, 0, :], gT[:, 0:P], b2_s[:, :], start=True, stop=True)
                    pe.matmul(M[:, 1, :], gT[:, P:2 * P], b2_s[:, :], start=True, stop=True).then_inc(m_ready, 1)

            def up_tile(i, e, f):
                kind = "F01" if f < 2 else "F23"
                if f % 2 == 0:
                    pe.wait_ge(w1_in, 16 * (NE * (i - 1) + e + 1))
                    pe.wait_ge(m_taken, piece_no(i, kind, e))
                for k in range(2):
                    last = pe.matmul(M[:, f % 2, :], w1s[:, k, f * P:(f + 1) * P], h2T[:, k, :], start=(k == 0), stop=(k == 1))
                if f % 2 == 1:
                    last.then_inc(m_ready, 1)

            def down_part(i, e, part):
                t, f = part // NF, part % NF
                if part == 0:
                    pe.wait_ge(w2_in, 16 * (NE * (i - 1) + e + 1))
                    pe.wait_ge(m_taken, piece_no(i, "Y", e))
                last = pe.matmul(M[:, t, :], hid[:, f, t * P:(t + 1) * P], w2s[:, f, :], start=(f == 0), stop=(f == NF - 1))
                if part == 2 * NF - 1:
                    last.then_inc(m_ready, 1)

            def scores(i, first, slot, parity):
                n = SLOTS * i + NCHUNK * first + slot
                at_start = isinstance(first, int) and first == 0 and slot < 2
                if due(n - 1 if at_start else n - 2):
                    pe.wait_ge(exp_done, n - 1 if at_start else n - 2)
                tile = first + slot // NCHUNK
                for h in range(2):
                    q0 = (slot % NCHUNK) * CHUNK + h * 512
                    last = pe.matmul(S[score_buffer(first, slot)][:, h, :], kT[parity][:, tile_cols(tile)],
                                     qT[parity][:, q0:q0 + 512], start=True, stop=True)
                last.then_inc(scores_ready, 1)

            def weighted(B, tiles, bset, unit, opens, closes):
                j, half, e = unit // 4, unit // 2 % 2, unit % 2
                if unit <= 1:
                    pe.wait_ge(wsum_ready, B + 1)
                for q in range(4):
                    a0 = ((4 * half + q) * 2 + e) * ROWS
                    last = pe.matmul(R[32 * q:32 * q + 32, half, :], wsum[bset][:, j, 2 * half + q // 2, DH * (1 - e):DH * (3 - e)],
                                     E[bset][j][:, a0:a0 + ROWS], start=(opens and unit == 0),
                                     stop=(closes and j == tiles - 1 and e == 1), skip_group_check=True)
                if unit % 4 == 3:
                    last.then_inc(r_tile_done, 1)

            def add_pool_sum(i):
                pe.wait_ge(pool_steps, POOL_STEPS * i)
                for q in range(4):
                    last = pe.matmul(R[32 * q:32 * q + 32, 0, :], ones_col[:, :], pool_sum[:, q * ROWS:(q + 1) * ROWS],
                                     start=False, stop=False, skip_group_check=True)
                last.then_inc(pool_sum_used, 1)

            pe.wait_ge(c_silu, 1)
            for b in range(NB):
                for n in range(3):
                    at = 3 * b + n
                    for k in range(2):
                        last = pe.matmul(S[at // 2][:, at % 2, :], cwide[:, k, b, :], wmod_s[:, k, n * 512:(n + 1) * 512],
                                         start=(k == 0), stop=(k == 1))
            last.then_inc(mod_ready, 1)
            pe.wait_ge(consts_ready, 1)
            for kind in PRE_PIECES:
                for half in range(1 if kind == "h1T" else 2):
                    pre_piece(-1, kind, half)
            pe.wait_ge(rows_ready, 1)

            PRE_AT = {(0, 7): ("h1T", 0), (1, 6): ("Q", 0), (1, 7): ("Q", 1), (1, 9): ("K", 0), (1, 10): ("K", 1),
                      (2, 2): ("V", 0), (2, 3): ("V", 1)}
            POST_AT = {(1, 3): ("Wo", 0), (1, 4): ("Wo", 1), (1, 11): ("h2T", 0), (2, 1): ("logits", 0),
                       (2, 7): ("gT", 0), (2, 9): ("b2", 0)}
            UNITS = {6: (1, 2), 11: (3, 5)}
            LATE_UNITS = {0: (6, 7), 3: (9, 10, 11)}
            HEAD_UNITS = ({4: (0, 1), 5: (2, 3), 6: (4, 5), 7: (6, 7)},
                          {5: (0, 1), 8: (2, 3), 11: (4, 5)},
                          {5: (0, 1), 8: (2, 3), 10: (4, 5), 11: (8,)})
            HEAD_LATE = (LATE_UNITS, {0: (8, 9), 1: (10, 11)}, {0: (6, 7)})
            POOL_SUM_SLOT = 7
            UP_AT = {1: 0, 2: 1, 4: 2, 5: 3}
            DOWN_AT = {7: (0, 1), 8: (2, 3), 9: (4, 5), 10: (6, 7)}

            def pe_block(i, parity, pre, att, post):
                if att:
                    pe.wait_ge(qk_in, 16 * 2 * len(TERMS) * (i + 1))
                for b, (first, tiles) in enumerate(HEAD):
                    B = batch_index(i, b)
                    before = HEAD[b - 1][1] if b > 0 else 3
                    before2 = HEAD[b - 2][1] if b > 1 else 3
                    for slot in range(NCHUNK * tiles):
                        if att:
                            scores(i, first, slot, parity)
                        if (b < 2 and post) or (b == 2 and att):
                            for unit in HEAD_LATE[b].get(slot, ()):
                                weighted(B - 2, before2, set_of(parity, b), unit, False, b == 1)
                        if (b == 0 and post) or (b > 0 and att):
                            if b == 1 and slot == 5 and post:
                                pe.wait_ge(r_taken, i)
                            if b == 0 and slot == POOL_SUM_SLOT:
                                add_pool_sum(i)
                            for unit in HEAD_UNITS[b].get(slot, ()):
                                weighted(B - 1, before, set_of(parity, b - 1), unit, b == 1, False)
                        if post and (b, slot) in POST_AT:
                            post_piece(i, *POST_AT[b, slot], parity)
                        if pre and (b, slot) in PRE_AT:
                            pre_piece(i, *PRE_AT[b, slot])
                with pe.Fori(0, BODY_ITERS) as it:
                    for h in range(2):
                        b = len(HEAD) + 2 * it + h
                        B = batch_index(i, b)
                        bset = set_of(parity, len(HEAD) + h)
                        first = BODY_FIRST + 6 * it + 3 * h
                        for slot in range(NCHUNK * 3):
                            if att:
                                scores(i, first, slot, parity)
                                for unit in LATE_UNITS.get(slot, ()):
                                    weighted(B - 2, 3, bset, unit, False, False)
                                for unit in UNITS.get(slot, ()):
                                    weighted(B - 1, 3, 1 - bset, unit, False, False)
                            if post and slot in UP_AT:
                                up_tile(i, 2 * it + h, UP_AT[slot])
                            if post:
                                for part in DOWN_AT.get(slot, ()):
                                    down_part(i, 2 * it + h, part)

            over_blocks(pe, pe_block)


        @block.scalar
        def _(act):
            def exp_chunk(i, first, slot, b, bset):
                j, ch = slot // NCHUNK, slot % NCHUNK
                if ch == 0:
                    last_use = TILES * i + first + j - (5 if isinstance(b, int) and b > 0 else 6)
                    if due(last_use + 1):
                        act.wait_ge(r_tile_done, last_use + 1)
                    if not isinstance(b, int):
                        act.wait_ge(pool_steps, POOL_STEPS * i + 3 * (b - 3) + j + 1)
                    elif b == 0 and due(i):
                        act.wait_ge(pool_steps, POOL_STEPS * i - 2 + j)
                    elif b == 2 and j == 2 and due(i):
                        act.wait_ge(pool_steps, POOL_STEPS * i)
                act.wait_ge(max_ready, SLOTS * i + NCHUNK * first + slot + 1)
                nc.scalar.activation(E[bset][j][:, ch * CHUNK:(ch + 1) * CHUNK].rearrange("p (h n) -> p h n", h=2),
                                     S[score_buffer(first, slot)][:, :, :], ACT.Exp, bias=nmax[bset][:, j, ch:ch + 1],
                                     accum_out=zc[bset][:, j, ch:ch + 1]).then_inc(exp_done, 1)

            def exp_maxima(i, b, tiles, bset):
                act.wait_ge(dmax_ready, batch_index(i, b) + 1)
                nc.scalar.activation(emax[bset][:, 0:tiles, :], dmax[bset][:, 0:tiles, :], ACT.Exp).then_inc(emax_ready, 1)

            def pre_take(i, kind, parity):
                act.wait_ge(m_ready, piece_no(i, kind) + 1)
                if kind == "h1T":
                    last = nc.scalar.activation(h1T[:, :, :], M[:, :, :], ACT.Copy)
                else:
                    if kind != "V":
                        if due(i + 1):
                            act.wait_ge(q_split if kind == "Q" else k_split, i + 1)
                    dst, bias, scale = {"Q": (qf, bq_c, 1.0 / D), "K": (kf, bk_c, 1.0), "V": (vT[parity], bv_c, 1.0)}[kind]
                    for m in range(2):
                        last = nc.scalar.activation(dst[:, m, :], M[:, m, :], ACT.Identity, bias=bias[:, m:m + 1], scale=scale)
                last.then_inc(m_taken, 1)

            def post_take(i, kind):
                if kind == "gate exp":
                    act.wait_ge(lgd_ready, i)
                    nc.scalar.activation(lge[:, :, :], lgd[:, :, :], ACT.Exp).then_inc(lge_ready, 1)
                    return
                act.wait_ge(m_ready, piece_no(i, kind) + 1)
                if kind == "h2T":
                    nc.scalar.activation(h2T[:, :, :], M[:, :, :], ACT.Copy).then_inc(m_taken, 1)
                else:
                    nc.scalar.activation(gT[:, :], M[0:NE, 0, :], ACT.Copy).then_inc(m_taken, 1)

            def hidden_take(i, kind, e):
                act.wait_ge(m_ready, piece_no(i, kind, e) + 1)
                for n in range(2):
                    f = (0 if kind == "F01" else 2) + n
                    last = nc.scalar.activation(hid[:, f, :], M[:, n, :], ACT.Relu, bias=b1_c[:, e, f:f + 1])
                last.then_inc(m_taken, 1)

            act.wait_ge(consts_in, 16 * CONST_LOADS)
            nc.scalar.activation(csig, cT, ACT.Exp, scale=-1.0).then_inc(c_exp, 1)
            act.wait_ge(rows_ready, 1)
            for kind in PRE_PIECES:
                pre_take(-1, kind, 0)

            PRE_AT = {(0, 7): "h1T", (1, 6): "Q", (1, 9): "K", (2, 2): "V"}
            POST_AT = {(1, 10): "h2T", (2, 1): "gate exp", (2, 6): "gT"}
            EXPERT_AT = {1: "F01", 4: "F23"}

            def act_block(i, parity, pre, att, post):
                for b, (first, tiles) in enumerate(HEAD):
                    for slot in range(NCHUNK * tiles):
                        if att:
                            exp_chunk(i, first, slot, b, set_of(parity, b))
                        if post and (b, slot) in POST_AT:
                            post_take(i, POST_AT[b, slot])
                        if pre and (b, slot) in PRE_AT:
                            pre_take(i, PRE_AT[b, slot], 1 - parity)
                    if att:
                        exp_maxima(i, b, tiles, set_of(parity, b))
                with act.Fori(0, BODY_ITERS) as it:
                    for h in range(2):
                        b = len(HEAD) + 2 * it + h
                        bset = set_of(parity, len(HEAD) + h)
                        for slot in range(NCHUNK * 3):
                            if att:
                                exp_chunk(i, BODY_FIRST + 6 * it + 3 * h, slot, b, bset)
                            if post and slot in EXPERT_AT:
                                hidden_take(i, EXPERT_AT[slot], 2 * it + h)
                        if att:
                            exp_maxima(i, b, 3, bset)

            over_blocks(act, act_block)

        @block.vector
        def _(dve):
            def chunk_max(i, first, slot, bset):
                n = SLOTS * i + NCHUNK * first + slot + 1
                dve.wait_ge(scores_ready, n)
                dve.tensor_reduce(nmax[bset][:, slot // NCHUNK, slot % NCHUNK:slot % NCHUNK + 1],
                                  S[score_buffer(first, slot)][:, :, :], AX.XY, ALU.max, negate=True).then_inc(max_ready, 1)
                return n

            def all_max(done, tiles, bset):
                dve.wait_ge(max_ready, done)
                dve.tensor_reduce(nall[bset][:, 0:tiles], nmax[bset][:, 0:tiles, :], AX.X, ALU.min).then_inc(nall_ready, 1)

            def max_differences(B, tiles, bset):
                dve.wait_ge(nall_ready, B + 1)
                dve.tensor_tensor(dmax[bset][:, 0:tiles, :], nall[bset][:, 0:tiles].unsqueeze(2).to_broadcast([P, tiles, NCHUNK]),
                                  nmax[bset][:, 0:tiles, :], ALU.subtract).then_inc(dmax_ready, 1)

            def denominators(B, tiles, bset):
                dve.wait_ge(emax_ready, B + 1)
                dve.tensor_tensor(zz[bset][:, 0:tiles, :], zc[bset][:, 0:tiles, :], emax[bset][:, 0:tiles, :], ALU.mult).then_inc(zz_ready, 1)
                dve.wait_ge(zz_ready, B + 1)
                dve.tensor_reduce(zsum[bset][:, 0:tiles], zz[bset][:, 0:tiles, :], AX.X, ALU.add).then_inc(zsum_ready, 1)
                dve.wait_ge(zsum_ready, B + 1)
                dve.reciprocal(rz[bset][:, 0:tiles], zsum[bset][:, 0:tiles]).then_inc(rz_ready, 1)

            def layer_stats(name, src, n):
                st, mv, _, _ = ln[name]
                bn_done, mean_ready = stats[name][0:2]
                for t in range(2):
                    dve.bn_stats(st[:, t, :], src[:, t, :]).then_inc(bn_done, 1)
                dve.wait_ge(bn_done, 2 * (n + 1))
                on_its_own(dve, 2 * (n + 1))
                for t in range(2):
                    dve.bn_aggr(mv[:, t, :], st[:, t, :]).then_inc(mean_ready, 1)

            def normalise(name, dst, src, n):
                _, mv, _, rs = ln[name]
                dve.wait_ge(stats[name][1], 2 * (n + 1))
                dve.wait_ge(stats[name][3], n + 1)
                for t in range(2):
                    dve.tensor_scalar(dst[:, t, :], src[:, t, :], mv[:, t, 0:1], rs[:, t:t + 1],
                                      ALU.subtract, ALU.mult).then_inc(stats[name][4], 1)

            def round_part(i, part):
                if part == HI:
                    dve.wait_ge(m_taken, piece_no(i, "K") + 1)
                    if due(i + 1):
                        dve.wait_ge(k_parts_out, 16 * (i + 1))
                        on_its_own(dve, i)
                    dve.tensor_copy(qparts[:, part, :, :], qf[:, :, :])
                    dve.tensor_copy(kparts[:, part, :, :], kf[:, :, :]).then_inc(hi_ready, 1)
                else:
                    dve.wait_ge(rest_ready, i + 2)
                    on_its_own(dve, i)
                    dve.tensor_copy(qparts[:, part, :, :], qf[:, :, :])
                    dve.tensor_copy(kparts[:, part, :, :], kf[:, :, :]).then_inc(mid_ready, 1)

            def residual(i, parity):
                at = piece_no(i, "Wo") + 1
                dve.wait_ge(x1_biased, i)
                dve.wait_ge(m_ready, at)
                dve.tensor_tensor(y[:, :, :], M[:, :, :], rows_of_batch(ga_r, i - 1), ALU.mult).then_inc(m_taken, 1)
                dve.wait_ge(m_taken, at)
                dve.tensor_tensor(x1[1 - parity][:, :, :], x1[1 - parity][:, :, :], y[:, :, :], ALU.add).then_inc(x1_ready, 1)
                dve.wait_ge(x1_ready, i)
                layer_stats("two", x1[1 - parity], i - 1)

            def logits(i):
                at = piece_no(i, "logits") + 1
                dve.wait_ge(m_ready, at)
                dve.tensor_tensor(lg[:, :, :], M[:, :, 0:NE], bg_r[:, :].unsqueeze(1).to_broadcast([P, 2, NE]), ALU.add).then_inc(m_taken, 1)
                dve.wait_ge(m_taken, at)
                link = Chain(dve, gate_link, GATE_LINKS * (i - 1))
                link(dve.tensor_reduce(top[:, :], lg[:, :, :], AX.X, ALU.max))
                dve.tensor_tensor(lgd[:, :, :], lg[:, :, :], top[:, :].unsqueeze(2).to_broadcast([P, 2, NE]),
                                  ALU.subtract).then_inc(lgd_ready, 1)

            def routing(i):
                link = Chain(dve, gate_link, GATE_LINKS * (i - 1) + 1)
                other = lg[:, :, :].unsqueeze(2).to_broadcast([P, 2, NE, NE])
                own = lg[:, :, :].unsqueeze(3).to_broadcast([P, 2, NE, NE])
                before = earlier[:, :, :].unsqueeze(1).to_broadcast([P, 2, NE, NE])
                dve.tensor_tensor(gt[:, :, :, :], other, own, ALU.is_gt)
                link(dve.tensor_tensor(eq[:, :, :, :], other, own, ALU.is_equal))
                link(dve.tensor_tensor(eq[:, :, :, :], eq[:, :, :, :], before, ALU.mult))
                link(dve.tensor_tensor(gt[:, :, :, :], gt[:, :, :, :], eq[:, :, :, :], ALU.add))
                link(dve.tensor_reduce(rank[:, :, :], gt[:, :, :, :], AX.X, ALU.add))
                dve.wait_ge(lge_ready, i)
                link(dve.scalar_tensor_tensor(chosen[:, :, :], rank[:, :, :], 1.5, lge[:, :, :], ALU.is_lt, ALU.mult))
                link(dve.tensor_reduce(gsum[:, :], chosen[:, :, :], AX.X, ALU.add))
                link(dve.reciprocal(grec[:, :], gsum[:, :]))
                dve.tensor_tensor(gate[:, :, :], chosen[:, :, :], grec[:, :].unsqueeze(2).to_broadcast([P, 2, NE]),
                                  ALU.mult).then_inc(gate_ready, 1)

            def start_y(i):
                dve.wait_ge(m_ready, piece_no(i, "b2") + 1)
                dve.tensor_tensor(y[:, :, :], M[:, :, :], h2[:, :, :], ALU.add).then_inc(m_taken, 1)

            def add_expert(i, e):
                at = piece_no(i, "Y", e) + 1
                dve.wait_ge(m_taken, at - 3 if not isinstance(e, int) else at - 1)
                dve.wait_ge(m_ready, at)
                for t in range(2):
                    last = dve.scalar_tensor_tensor(y[:, t, :], M[:, t, :], gate[:, t, bass.ds(e, 1)], y[:, t, :], ALU.mult, ALU.add)
                last.then_inc(m_taken, 1)

            link = Chain(dve, c_link, 0)
            dve.wait_ge(c_exp, 1)
            link(dve.tensor_scalar(csig, csig, 1.0, None, ALU.add))
            link(dve.reciprocal(csil, csig))
            link(dve.tensor_tensor(csil, csil, cT, ALU.mult))
            for k in range(2):
                for b in range(NB):
                    last = dve.tensor_copy(cwide[:, k, b, :], csil[:, k, b:b + 1].to_broadcast([P, P]))
            last.then_inc(c_silu, 1)
            dve.wait_ge(x_in, 16)
            layer_stats("one", xin, 0)
            normalise("one", xin, xin, 0)
            dve.wait_ge(mod_ready, 1)
            link = Chain(dve, mod_link, 0)
            for b in range(NB):
                for n in range(3):
                    at = 3 * b + n
                    last = dve.tensor_copy(modr[b][:, n * 512:(n + 1) * 512], S[at // 2][:, at % 2, :])
            link(last)
            for b in range(NB):
                part = [modr[b][:, n * D:(n + 1) * D] for n in range(6)]
                dve.tensor_copy(sa_r[:, b, :], part[0])
                dve.tensor_scalar(c1a_r[:, b, :], part[1], 1.0, None, ALU.add)
                dve.tensor_copy(sb_r[:, b, :], part[3])
                dve.tensor_scalar(c1b_r[:, b, :], part[4], 1.0, None, ALU.add)
                for g, at in ((part[2], 0), (part[5], 1)):
                    link(dve.tensor_scalar(scr[:, at, :], g, -1.0, None, ALU.mult))
                    link(dve.tensor_tensor(scr[:, at, :], scr[:, at, :], g, ALU.max))
                    link(dve.tensor_scalar(scr[:, at, :], scr[:, at, :], 0.25, None, ALU.max))
                    link(dve.tensor_scalar(scr2[:, at, :], g, 0.0, 2.0, ALU.is_ge, ALU.mult))
                    link(dve.tensor_scalar(scr2[:, at, :], scr2[:, at, :], -1.0, None, ALU.add))
                    link(dve.tensor_tensor(scr3[:, at, :], scr[:, at, :], scr2[:, at, :], ALU.mult))
                dve.tensor_copy(ga_r[:, b, :], scr3[:, 0, :])
                dve.tensor_tensor(gabo_r[:, b, :], scr3[:, 0, :], bo_r, ALU.mult)
                dve.tensor_tensor(gscale_r[:, b, :], scr3[:, 1, :], gamma_r, ALU.mult)
                link(dve.tensor_tensor(gshift_r[:, b, :], scr3[:, 1, :], beta_r, ALU.mult))
            dve.tensor_scalar(bq_c[:, :], bq_c[:, :], 1.0 / D, None, ALU.mult).then_inc(rows_ready, 1)
            dve.wait_ge(rows_ready, 1)
            round_part(-1, HI)
            round_part(-1, MID)

            def dve_block(i, parity, pre, att, post):
                for b, (first, tiles) in enumerate(HEAD):
                    prev = 3 if b == 0 else HEAD[b - 1][1]
                    done = 0
                    for slot in range(NCHUNK * tiles):
                        if att:
                            done = chunk_max(i, first, slot, set_of(parity, b))
                        if slot == 2 and ((b == 0 and post) or (b > 0 and att)):
                            denominators(batch_index(i, b) - 1, prev, set_of(parity, b - 1))
                        if pre and (b, slot) == (0, 0):
                            dve.wait_ge(x_in, 16 * (i + 2))
                            layer_stats("one", xin, i + 1)
                        if pre and (b, slot) == (0, 1):
                            normalise("one", xin, xin, i + 1)
                        if post and (b, slot) == (1, 1):
                            dve.wait_ge(r_tile_done, TILES * i)
                            dve.tensor_tensor(vT[1 - parity][:, :, :], R[:, :, :], vT[1 - parity][:, :, :], ALU.mult).then_inc(r_taken, 1)
                        if post and (b, slot) == (1, 4):
                            residual(i, parity)
                        if post and (b, slot) == (1, 6):
                            normalise("two", h2, x1[1 - parity], i - 1)
                        if post and (b, slot) == (2, 1):
                            logits(i)
                        if post and (b, slot) == (2, 3):
                            routing(i)
                        if pre and (b, slot) == (2, 0):
                            round_part(i, HI)
                        if pre and (b, slot) == (2, 7):
                            round_part(i, MID)
                        if post and (b, slot) == (2, 9):
                            start_y(i)
                    if att:
                        all_max(done, tiles, set_of(parity, b))
                        max_differences(batch_index(i, b), tiles, set_of(parity, b))
                with dve.Fori(0, BODY_ITERS) as it:
                    for h in range(2):
                        b = len(HEAD) + 2 * it + h
                        bset = set_of(parity, len(HEAD) + h)
                        done = 0
                        for slot in range(NCHUNK * 3):
                            if att:
                                done = chunk_max(i, BODY_FIRST + 6 * it + 3 * h, slot, bset)
                            if att and slot == 2:
                                denominators(batch_index(i, b) - 1, 3, 1 - bset)
                            if post and slot == 11:
                                add_expert(i, 2 * it + h)
                        if att:
                            all_max(done, 3, bset)
                            max_differences(batch_index(i, b), 3, bset)
                if post:
                    dve.wait_ge(m_taken, piece_no(i, "Y", NE - 1) + 1)
                    layer_stats("out", y, i - 1)
                    _, mv, _, rs = ln["out"]
                    dve.wait_ge(stats["out"][1], 2 * i)
                    dve.wait_ge(x1_shifted, i)
                    for t in range(2):
                        dve.scalar_tensor_tensor(y[:, t, :], y[:, t, :], mv[:, t, 0:1], row_of_batch(gscale_r, i - 1),
                                                 ALU.subtract, ALU.mult).then_inc(out_scaled, 1)
                    dve.wait_ge(out_scaled, 2 * i)
                    dve.wait_ge(stats["out"][3], i)
                    for t in range(2):
                        last = dve.scalar_tensor_tensor(y[:, t, :], y[:, t, :], rs[:, t:t + 1], x1[1 - parity][:, t, :],
                                                        ALU.mult, ALU.add)
                    last.then_inc(out_ready, 1)

            over_blocks(dve, dve_block)

        @block.gpsimd
        def _(pool):
            def weights(B, first, tiles, bset):
                pool.wait_ge(rz_ready, B + 1)
                if due(first - 3):
                    pool.wait_ge(r_tile_done, first - 3)
                pool.tensor_tensor(wsum[bset][:, 0:tiles, :, DH:2 * DH],
                                   emax[bset][:, 0:tiles, :].unsqueeze(3).to_broadcast([P, tiles, NCHUNK, DH]),
                                   rz[bset][:, 0:tiles].unsqueeze(2).unsqueeze(3).to_broadcast([P, tiles, NCHUNK, DH]),
                                   ALU.mult).then_inc(wsum_ready, 1)

            def clear_sum(i):
                if due(i):
                    pool.wait_ge(pool_sum_used, i)
                    on_its_own(pool, i)
                pool.memset(pool_sum[:, :], 0.0).then_inc(pool_steps, 3)

            def add_tile(i, n, B, j, bset):
                step = POOL_STEPS * i + 3 + n
                part = E[bset][j][:, 0:2 * QUARTER].rearrange("p (c g e r) -> p c g e r", c=2, g=2, e=2)[:, :, :, 0, :]
                weight = wsum[bset][:, j, 0:2, DH].unsqueeze(2).unsqueeze(3).to_broadcast([P, 2, 2, ROWS])
                sums = pool_sum[:, :].rearrange("p (c g r) -> p c g r", c=2, g=2)
                if j == 0:
                    pool.wait_ge(wsum_ready, B + 1)
                pool.tensor_tensor(part, part, weight, ALU.mult).then_inc(pool_scaled, 1)
                pool.wait_ge(pool_scaled, (POOL_STEPS - 3) * i + n + 1)
                pool.wait_ge(pool_steps, step)
                pool.tensor_tensor(sums, sums, part, ALU.add).then_inc(pool_steps, 1)

            def inverse_deviation(name, n):
                _, mv, ve, rs = ln[name]
                _, mean_ready, ve_ready, rstd_ready, _ = stats[name]
                pool.wait_ge(mean_ready, 2 * (n + 1))
                on_its_own(pool, 2 * (n + 1))
                pool.tensor_scalar(ve[:, :], mv[:, :, 1], EPS, None, ALU.add).then_inc(ve_ready, 1)
                pool.wait_ge(ve_ready, n + 1)
                pool.tensor_tensor(rs[:, :], ve[:, :], mhalf[:, :], ALU.pow).then_inc(rstd_ready, 1)

            def scale_rows(name, buf, scale_r, n, scaled):
                pool.wait_ge(stats[name][4], 2 * (n + 1))
                pool.tensor_tensor(buf[:, :, :], buf[:, :, :], rows_of_batch(scale_r, n), ALU.mult).then_inc(scaled, 1)

            def shift_rows(buf, shift_r, n, scaled, ready):
                pool.wait_ge(scaled, n + 1)
                pool.tensor_tensor(buf[:, :, :], buf[:, :, :], rows_of_batch(shift_r, n), ALU.add).then_inc(ready, 1)

            def take_off_high(i):
                pool.wait_ge(hi_ready, i + 2)
                pool.tensor_tensor(qf[:, :, :], qf[:, :, :], qparts[:, HI, :, :], ALU.subtract)
                pool.tensor_tensor(kf[:, :, :], kf[:, :, :], kparts[:, HI, :, :], ALU.subtract).then_inc(rest_ready, 1)

            def low_parts(i):
                pool.wait_ge(mid_ready, i + 2)
                pool.tensor_tensor(qparts[:, LO, :, :], qf[:, :, :], qparts[:, MID, :, :], ALU.subtract).then_inc(q_split, 1)
                pool.tensor_tensor(kparts[:, LO, :, :], kf[:, :, :], kparts[:, MID, :, :], ALU.subtract).then_inc(k_split, 1)

            def bias_residual(i, parity):
                pool.wait_ge(x1_in, 16 * i)
                pool.tensor_tensor(x1[1 - parity][:, :, :], x1[1 - parity][:, :, :], rows_of_batch(gabo_r, i - 1), ALU.add).then_inc(x1_biased, 1)

            def shift_residual(i, parity):
                pool.tensor_tensor(x1[1 - parity][:, :, :], x1[1 - parity][:, :, :], rows_of_batch(gshift_r, i - 1), ALU.add).then_inc(x1_shifted, 1)

            pool.memset(mhalf[:, :], -0.5)
            pool.memset(wsum[0][:, :, :, :], 0.0)
            pool.memset(wsum[1][:, :, :, :], 0.0)
            pool.memset(ones_col[:, :], 0.0)
            pool.memset(earlier[:, :, :], 1.0)
            pool.memset(ident[:, :], 0.0).then_inc(ident_zeroed, 1)
            pool.wait_ge(ident_zeroed, 1)
            pool.affine_select(out=earlier[:, :, :], in_=earlier[:, :, :], compare_op=ALU.is_gt, fill=0.0, base=0,
                               pattern=[[1, NE], [-1, NE]], channel_multiplier=0)
            pool.memset(ones_col[:, 0:DH], 1.0)
            pool.affine_select(out=ident[:, :], in_=ident[:, :], compare_op=ALU.not_equal, fill=1.0, base=0,
                               pattern=[[-1, P]], channel_multiplier=1).then_inc(consts_ready, 1)
            pool.wait_ge(consts_ready, 1)
            inverse_deviation("one", 0)
            pool.wait_ge(rows_ready, 1)
            scale_rows("one", xin, c1a_r, 0, h1_scaled)
            shift_rows(xin, sa_r, 0, h1_scaled, h1_ready)
            take_off_high(-1)
            low_parts(-1)

            def pool_block(i, parity, pre, att, post):
                for b, (first, tiles) in enumerate(HEAD):
                    before = HEAD[b - 1][1] if b > 0 else 3
                    B = batch_index(i, b)
                    weigh = (b == 0 and post) or (b > 0 and att)
                    if b == 0 and pre:
                        inverse_deviation("one", i + 1)
                    if b == 0 and pre:
                        scale_rows("one", xin, c1a_r, i + 1, h1_scaled)
                    if weigh:
                        weights(B - 1, TILES * i + first - before, before, set_of(parity, b - 1))
                    if b == 0 and pre:
                        shift_rows(xin, sa_r, i + 1, h1_scaled, h1_ready)
                    if b == 0 and post:
                        bias_residual(i, parity)
                    if b == 1 and post:
                        inverse_deviation("two", i - 1)
                        scale_rows("two", h2, c1b_r, i - 1, h2_scaled)
                        shift_rows(h2, sb_r, i - 1, h2_scaled, h2_ready)
                        shift_residual(i, parity)
                    if b == 2 and pre:
                        take_off_high(i)
                        low_parts(i)
                    if b == 1 and att:
                        clear_sum(i)
                if att:
                    with pool.Fori(0, BODY_ITERS) as it:
                        for h in range(2):
                            b = len(HEAD) + 2 * it + h
                            bset = set_of(parity, len(HEAD) + h)
                            weights(batch_index(i, b) - 1, TILES * i + BODY_FIRST + 6 * it + 3 * h - 3, 3, 1 - bset)
                            for j in range(3):
                                add_tile(i, 3 * (2 * it + h) + j, batch_index(i, b) - 1, j, 1 - bset)
                if post:
                    inverse_deviation("out", i - 1)

            over_blocks(pool, pool_block)


_INS = ['L0_attn_X_embed', 'L0_attn_Wq', 'L0_attn_bq', 'L0_attn_Wk', 'L0_attn_bk', 'L0_attn_Wv', 'L0_attn_bv', 'L0_attn_Wo', 'L0_attn_bo', 'L0_ffn_Wg', 'L0_ffn_bg', 'L0_ffn_W1', 'L0_ffn_b1', 'L0_ffn_W2', 'L0_ffn_b2', 'L0_ffn_gamma', 'L0_ffn_beta', 'L0_c', 'L0_wmod']
_OUT = ((2, 4096, 256), "float32")


def kernel(**inputs):
    import numpy as _np
    import concourse.bacc as _bacc
    from concourse import mybir as _mybir
    from concourse.bass_utils import run_bass_kernel_spmd as _run

    nc = _bacc.Bacc("TRN2", target_bir_lowering=False, num_devices=1)
    arrays, args = {}, []
    for name in _INS:
        a = _np.ascontiguousarray(inputs[name])
        arrays[f"in_{name}"] = a
        args.append(nc.dram_tensor(f"in_{name}", a.shape, _mybir.dt.from_np(a.dtype), kind="ExternalInput").ap())
    out = nc.dram_tensor("out", _OUT[0], _mybir.dt.from_np(_np.dtype(_OUT[1])), kind="ExternalOutput").ap()
    adaln_layer(nc, *args, out)
    r = _run(nc, [arrays], core_ids=[0])
    return r.results[0]["out"]
```

```python
from contextlib import ExitStack

import concourse.bass as bass
from concourse import mybir

F32 = mybir.dt.float32
BF16 = mybir.dt.bfloat16
ALU = mybir.AluOpType
ACT = mybir.ActivationFunctionType
AX = mybir.AxisListType

P = 128
ROWS = 256
D = 256
DH = 16
GROUPS = D // DH
POS = ROWS * GROUPS
CHUNK = 1024
NCHUNK = POS // CHUNK
TILES = POS // P
NE = 8
FF = 512
NF = FF // P
NB = 2
BLOCKS = NB * 4096 // ROWS
EPS = 1e-5
SLOTS = NCHUNK * TILES
QUARTER = POS // 4

HEAD = ((0, 2), (2, 3), (5, 3))
BODY_FIRST = 8
ROUND = 4
BODY_ITERS = NE // ROUND
BATCHES = len(HEAD) + NE
POOL_STEPS = 3 + 3 * NE

HI, MID, LO = range(3)
TERMS = ((HI, HI), (HI, MID), (MID, HI), (HI, LO), (LO, HI), (MID, MID), (MID, LO), (LO, MID))

PRE_PIECES = ("h1T", "Q", "K", "V")
HEAD_PIECES = ("Wo", "h1T", "Q", "K", "h2T", "logits", "V", "gT", "b2")
POST_PIECES = tuple(k for k in HEAD_PIECES if k not in PRE_PIECES)
EXPERT_PIECES = ("F01", "F23", "Y")
PER_BLOCK = len(HEAD_PIECES) + NE * len(EXPERT_PIECES)


GATE_LINKS = 8
CONST_LOADS = 19


def piece_no(i, kind, e=0):
    fixed = isinstance(i, int)
    if fixed and i < 1:
        return len(PRE_PIECES) * (i + 1) + PRE_PIECES.index(kind)
    base = 2 * len(PRE_PIECES) + PER_BLOCK * (i - 1)
    kinds = HEAD_PIECES
    if fixed and i >= BLOCKS - 1:
        kinds = POST_PIECES
        base = base - (len(PRE_PIECES) if i >= BLOCKS else 0)
    if kind in EXPERT_PIECES:
        return base + len(kinds) + len(EXPERT_PIECES) * e + EXPERT_PIECES.index(kind)
    return base + kinds.index(kind)


def adaln_layer(nc, x, Wq, bq, Wk, bk, Wv, bv, Wo, bo, Wg, bg, W1, b1, W2, b2, gamma, beta, c, wmod, out):
    with ExitStack() as ctx:
        def sb(name, shape, dt=F32):
            return ctx.enter_context(nc.sbuf_tensor(name, shape, dt))

        def ps(name, shape):
            return ctx.enter_context(nc.psum_tensor(name, shape, F32))

        def sem(name):
            return ctx.enter_context(nc.semaphore(name))

        E = [[sb(f"E{s}{j}", [P, POS]) for j in range(3)] for s in range(2)]
        qT = [sb(f"qT{s}", [P, POS], BF16) for s in range(2)]
        kT = [sb(f"kT{s}", [P, POS], BF16) for s in range(2)]
        wsum = [sb(f"wsum{s}", [P, 3, NCHUNK, 3 * DH]) for s in range(2)]
        pool_sum = sb("pool_sum", [P, QUARTER])
        ones_col = sb("ones_col", [P, 32])
        xin = sb("xin", [P, 2, D])
        h1T = sb("h1T", [P, 2, ROWS])
        qf = sb("qf", [P, 2, ROWS])
        kf = sb("kf", [P, 2, ROWS])
        qparts = sb("qparts", [P, 3, 2, ROWS], BF16)
        kparts = sb("kparts", [P, 3, 2, ROWS], BF16)
        vT = [sb(f"vT{s}", [P, 2, ROWS]) for s in range(2)]
        x1 = [sb(f"x1{s}", [P, 2, D]) for s in range(2)]
        h2 = sb("h2", [P, 2, D])
        h2T = sb("h2T", [P, 2, ROWS])
        y = sb("y", [P, 2, D])
        w1s = sb("w1s", [P, 2, FF])
        w2s = sb("w2s", [P, NF, D])
        hid = sb("hid", [P, NF, ROWS])
        wq_s, wk_s, wv_s, wo_s = (sb(n, [P, 2, D]) for n in ("wq_s", "wk_s", "wv_s", "wo_s"))
        wg_s = sb("wg_s", [P, 2, NE])
        b2_s = sb("b2_s", [NE, D])
        ident = sb("ident", [P, P])
        earlier = sb("earlier", [P, NE, NE])
        mod_names = ("sa", "c1a", "ga", "sb", "c1b", "gb")
        sa_r, c1a_r, ga_r, sb_r, c1b_r, gscale_r = (sb(f"{n}_r", [P, NB, D]) for n in mod_names)
        gabo_r = sb("gabo_r", [P, NB, D])
        gshift_r = sb("gshift_r", [P, NB, D])
        bg_r = sb("bg_r", [P, NE])
        bq_c, bk_c, bv_c = (sb(n, [P, 2]) for n in ("bq_c", "bk_c", "bv_c"))
        b1_c = sb("b1_c", [P, NE, NF])
        nmax = [sb(f"nmax{s}", [P, 3, NCHUNK]) for s in range(2)]
        zc = [sb(f"zc{s}", [P, 3, NCHUNK]) for s in range(2)]
        nall = [sb(f"nall{s}", [P, 3]) for s in range(2)]
        dmax = [sb(f"dmax{s}", [P, 3, NCHUNK]) for s in range(2)]
        emax = [sb(f"emax{s}", [P, 3, NCHUNK]) for s in range(2)]
        zz = [sb(f"zz{s}", [P, 3, NCHUNK]) for s in range(2)]
        zsum = [sb(f"zsum{s}", [P, 3]) for s in range(2)]
        rz = [sb(f"rz{s}", [P, 3]) for s in range(2)]
        ln = {n: (sb(f"st_{n}", [P, 2, 6]), sb(f"mv_{n}", [P, 2, 2]), sb(f"ve_{n}", [P, 2]), sb(f"rs_{n}", [P, 2]))
              for n in ("one", "two", "out")}
        mhalf = sb("mhalf", [P, 2])
        lg = sb("lg", [P, 2, NE])
        top = sb("top", [P, 2])
        lgd = sb("lgd", [P, 2, NE])
        lge = sb("lge", [P, 2, NE])
        gt = sb("gt", [P, 2, NE, NE])
        eq = sb("eq", [P, 2, NE, NE])
        rank = sb("rank", [P, 2, NE])
        chosen = sb("chosen", [P, 2, NE])
        gsum = sb("gsum", [P, 2])
        grec = sb("grec", [P, 2])
        gate = sb("gate", [P, 2, NE])
        gT = sb("gT", [NE, ROWS])

        S = [ps(f"S{n}", [P, 2, 512]) for n in range(3)]
        R = ps("R", [P, 2, ROWS])
        M = ps("M", [P, 2, ROWS])

        q_dram = nc.dram_tensor("q_dram", [3, GROUPS, DH, ROWS], BF16, kind="Internal").ap()
        k_dram = nc.dram_tensor("k_dram", [3, GROUPS, DH, ROWS], BF16, kind="Internal").ap()

        wmod_s = E[0][0][:, 0:2 * 1536].rearrange("p (k n) -> p k n", k=2)
        cT = E[0][1][:, 0:4].rearrange("p (k b) -> p k b", k=2)
        csig = E[0][1][:, 8:12].rearrange("p (k b) -> p k b", k=2)
        csil = E[0][1][:, 16:20].rearrange("p (k b) -> p k b", k=2)
        cwide = E[0][1][:, 1024:1024 + 4 * P].rearrange("p (k b m) -> p k b m", k=2, b=2)
        modr = [E[0][2][:, 0:1536], E[0][2][:, 1536:3072]]
        bo_r = E[1][0][:, 0:D]
        gamma_r = E[1][0][:, D:2 * D]
        beta_r = E[1][0][:, 2 * D:3 * D]
        scr = E[1][1][:, 0:2 * D].rearrange("p (b d) -> p b d", b=2)
        scr2 = E[1][1][:, 2 * D:4 * D].rearrange("p (b d) -> p b d", b=2)
        scr3 = E[1][1][:, 4 * D:6 * D].rearrange("p (b d) -> p b d", b=2)

        waits_passed = sem("waits_passed")
        consts_in = sem("consts_in")
        x_in, x1_in, w1_in, w2_in = sem("x_in"), sem("x1_in"), sem("w1_in"), sem("w2_in")
        q_parts_out, k_parts_out, qk_in, stored = sem("q_parts_out"), sem("k_parts_out"), sem("qk_in"), sem("stored")
        consts_ready = sem("consts_ready")
        ident_zeroed = sem("ident_zeroed")
        c_exp, c_silu, c_link = sem("c_exp"), sem("c_silu"), sem("c_link")
        mod_ready, mod_link, rows_ready = sem("mod_ready"), sem("mod_link"), sem("rows_ready")
        scores_ready, max_ready, exp_done = sem("scores_ready"), sem("max_ready"), sem("exp_done")
        nall_ready, dmax_ready, emax_ready, zz_ready = sem("nall_ready"), sem("dmax_ready"), sem("emax_ready"), sem("zz_ready")
        zsum_ready, rz_ready, wsum_ready = sem("zsum_ready"), sem("rz_ready"), sem("wsum_ready")
        r_tile_done, r_taken = sem("r_tile_done"), sem("r_taken")
        pool_scaled, pool_steps, pool_sum_used = sem("pool_scaled"), sem("pool_steps"), sem("pool_sum_used")
        m_ready, m_taken = sem("m_ready"), sem("m_taken")
        stats = {n: (sem(f"bn_{n}"), sem(f"mean_ready_{n}"), sem(f"ve_ready_{n}"), sem(f"rstd_ready_{n}"),
                     sem(f"norm_ready_{n}")) for n in ("one", "two", "out")}
        h1_scaled, h1_ready, h2_scaled, h2_ready = sem("h1_scaled"), sem("h1_ready"), sem("h2_scaled"), sem("h2_ready")
        hi_ready, rest_ready, mid_ready, q_split, k_split = (sem(n) for n in ("hi_ready", "rest_ready", "mid_ready", "q_split", "k_split"))
        x1_biased, x1_ready, x1_shifted = sem("x1_biased"), sem("x1_ready"), sem("x1_shifted")
        gate_link, lgd_ready, lge_ready, gate_ready = sem("gate_link"), sem("lgd_ready"), sem("lge_ready"), sem("gate_ready")
        out_scaled, out_ready = sem("out_scaled"), sem("out_ready")

        def due(count):
            return not isinstance(count, int) or count > 0

        def on_its_own(eng, count):
            if not isinstance(count, int):
                eng.sem_inc(waits_passed, 1)

        class Chain:
            def __init__(self, eng, s, done):
                self.eng, self.sem, self.done = eng, s, done

            def __call__(self, ins):
                self.done = self.done + 1
                ins.then_inc(self.sem, 1)
                self.eng.wait_ge(self.sem, self.done)
                on_its_own(self.eng, self.done)

        def over_blocks(eng, block):
            block(0, 0, pre=True, att=True, post=False, fin=False)
            block(1, 1, pre=True, att=True, post=True, fin=False)
            with eng.Fori(1, (BLOCKS - 2) // 2) as pair:
                block(2 * pair, 0, pre=True, att=True, post=True, fin=True)
                block(2 * pair + 1, 1, pre=True, att=True, post=True, fin=True)
            block(BLOCKS - 2, 0, pre=True, att=True, post=True, fin=True)
            block(BLOCKS - 1, 1, pre=False, att=True, post=True, fin=True)
            block(BLOCKS, 0, pre=False, att=False, post=True, fin=True)
            block(BLOCKS + 1, 1, pre=False, att=False, post=False, fin=True)

        def batch_index(i, b):
            return BATCHES * i + b

        def set_of(parity, b):
            return (parity + b) % 2

        def score_buffer(first, slot):
            at = NCHUNK * (first if isinstance(first, int) else BODY_FIRST) + slot
            return at % 3

        def tile_cols(tile):
            return bass.ts(tile, P)

        x_blocks = x.rearrange("b (n t p) d -> (b n) p t d", t=2, p=P)
        out_blocks = out.rearrange("b (n t p) d -> (b n) p t d", t=2, p=P)

        def rows_of_batch(rows, i):
            return rows[:, i // (BLOCKS // NB), :].unsqueeze(1).to_broadcast([P, 2, D])

        block = ctx.enter_context(nc.Block())

        @block.sync
        def _(sp):
            loads = [0]

            def cload(dst, src):
                loads[0] += 1
                sp.dma_start(dst, src, allow_slow_non_contiguous=True).then_inc(consts_in, 16)

            sp.dma_start(xin[:, :, :], x_blocks[0]).then_inc(x_in, 16)
            cload(wmod_s, wmod.rearrange("(k p) n -> p k n", p=P))
            for b in range(NB):
                for k in range(2):
                    cload(cT[:, k, b:b + 1], c[b:b + 1, k * P:(k + 1) * P].rearrange("b p -> p b"))
            for dst, src in ((wq_s, Wq), (wk_s, Wk), (wv_s, Wv), (wo_s, Wo), (wg_s, Wg)):
                cload(dst[:, :, :], src.rearrange("(k p) n -> p k n", p=P))
            cload(b2_s[:, :], b2)
            for dst, src, n in ((bo_r, bo, D), (gamma_r, gamma, D), (beta_r, beta, D), (bg_r[:, :], bg, NE)):
                cload(dst, src.rearrange("(a n) -> a n", a=1).to_broadcast([P, n]))
            for dst, src in ((bq_c, bq), (bk_c, bk), (bv_c, bv)):
                cload(dst[:, :], src.rearrange("(k p) -> p k", p=P))
            cload(b1_c[:, :, :], b1.rearrange("e (f p) -> p e f", p=P))

            def load_expert_up(e):
                sp.dma_start(w1s[:, :, :], W1[e].rearrange("(k p) f -> p k f", p=P)).then_inc(w1_in, 16)

            def load_expert_down(e):
                sp.dma_start(w2s[:, :, :], W2[e].rearrange("(f p) n -> p f n", p=P)).then_inc(w2_in, 16)

            assert loads[0] == CONST_LOADS, loads
            load_expert_up(0)
            load_expert_down(0)

            def move_parts(n, parity):
                if due(n):
                    sp.wait_ge(qk_in, 16 * 2 * len(TERMS) * n)
                    on_its_own(sp, n)
                sp.wait_ge(q_split, n + 1)
                on_its_own(sp, n + 1)
                sp.dma_start(q_dram.rearrange("s (t g) d r -> (g d) s t r", t=2), qparts[:, :, :, :]).then_inc(q_parts_out, 16)
                sp.wait_ge(k_split, n + 1)
                on_its_own(sp, n + 1)
                sp.dma_start(k_dram.rearrange("s (t g) d r -> (g d) s t r", t=2), kparts[:, :, :, :]).then_inc(k_parts_out, 16)
                if due(SLOTS * (n - 1)):
                    sp.wait_ge(scores_ready, SLOTS * (n - 1))
                    on_its_own(sp, SLOTS * (n - 1))
                sp.wait_ge(q_parts_out, 16 * (n + 1))
                on_its_own(sp, 16 * (n + 1))
                sp.wait_ge(k_parts_out, 16 * (n + 1))
                on_its_own(sp, 16 * (n + 1))
                for t, (a, b) in enumerate(TERMS):
                    strip = slice(DH * t, DH * (t + 1))
                    for dst, src, part in ((qT, q_dram, a), (kT, k_dram, b)):
                        sp.dma_start(dst[parity][strip, :].rearrange("d (g r) -> d g r", g=GROUPS),
                                     src[part].rearrange("g d r -> d g r")).then_inc(qk_in, 16)

            def load_x(n):
                sp.dma_start(xin[:, :, :], x_blocks[n]).then_inc(x_in, 16)

            move_parts(0, 0)
            load_x(1)

            def sp_block(i, parity, pre, att, post, fin):
                if post:
                    sp.dma_start(x1[1 - parity][:, :, :], x_blocks[i - 1]).then_inc(x1_in, 16)
                if fin:
                    sp.wait_ge(out_ready, i - 1)
                    on_its_own(sp, i - 1)
                    sp.dma_start(out_blocks[i - 2], y[:, :, :]).then_inc(stored, 16)
                if pre:
                    move_parts(i + 1, 1 - parity)
                    load_x((i + 2) % BLOCKS)
                if post:
                    def refill(e_done, e_next):
                        sp.wait_ge(m_ready, piece_no(i, "F23", e_done) + 1)
                        on_its_own(sp, piece_no(i, "F23", e_done) + 1)
                        load_expert_up(e_next)
                        sp.wait_ge(m_ready, piece_no(i, "Y", e_done) + 1)
                        on_its_own(sp, piece_no(i, "Y", e_done) + 1)
                        load_expert_down(e_next)

                    with sp.Fori(0, NE // 2 - 1) as it:
                        refill(2 * it, 2 * it + 1)
                        refill(2 * it + 1, 2 * it + 2)
                    refill(NE - 2, NE - 1)
                    if att:
                        refill(NE - 1, 0)

            over_blocks(sp, sp_block)
            sp.wait_ge(stored, 16 * BLOCKS)
            sp.wait_ge(q_parts_out, 16 * BLOCKS)
            sp.wait_ge(k_parts_out, 16 * BLOCKS)

        @block.tensor
        def _(pe):
            def bank_free(i, kind):
                if due(piece_no(i, kind)):
                    pe.wait_ge(m_taken, piece_no(i, kind))

            def transposes(dst, src):
                for k in range(2):
                    for t in range(2):
                        last = pe.transpose(dst[:, k, t * P:(t + 1) * P], src[:, t, k * P:(k + 1) * P], ident[:, :])
                return last

            def project(w, src, m):
                for k in range(2):
                    last = pe.matmul(M[:, m, :], w[:, k, m * P:(m + 1) * P], src[:, k, :], start=(k == 0), stop=(k == 1))
                return last

            def by_tokens(src, w, t, cols):
                for k in range(2):
                    last = pe.matmul(M[:, t, 0:cols], src[:, k, t * P:(t + 1) * P], w[:, k, :], start=(k == 0), stop=(k == 1))
                return last

            def pre_piece(i, kind, half):
                if half == 0:
                    bank_free(i, kind)
                if kind == "h1T":
                    pe.wait_ge(h1_ready, i + 2)
                    transposes(M, xin).then_inc(m_ready, 1)
                else:
                    if half == 0:
                        pe.wait_ge(m_taken, piece_no(i, "h1T") + 1)
                    last = project({"Q": wq_s, "K": wk_s, "V": wv_s}[kind], h1T, half)
                    if half == 1:
                        last.then_inc(m_ready, 1)

            def post_piece(i, kind, half, parity):
                if half == 0:
                    bank_free(i, kind)
                if kind == "Wo":
                    pe.wait_ge(r_taken, i)
                    last = by_tokens(vT[1 - parity], wo_s, half, D)
                    if half == 1:
                        last.then_inc(m_ready, 1)
                elif kind == "h2T":
                    pe.wait_ge(h2_ready, i)
                    transposes(M, h2).then_inc(m_ready, 1)
                elif kind == "logits":
                    pe.wait_ge(m_taken, piece_no(i, "h2T") + 1)
                    by_tokens(h2T, wg_s, 0, NE)
                    by_tokens(h2T, wg_s, 1, NE).then_inc(m_ready, 1)
                elif kind == "gT":
                    pe.wait_ge(gate_ready, i)
                    pe.transpose(M[0:NE, 0, 0:P], gate[:, 0, :], ident[:, :])
                    pe.transpose(M[0:NE, 0, P:2 * P], gate[:, 1, :], ident[:, :]).then_inc(m_ready, 1)
                elif kind == "b2":
                    pe.wait_ge(m_taken, piece_no(i, "gT") + 1)
                    pe.matmul(M[:, 0, :], gT[:, 0:P], b2_s[:, :], start=True, stop=True)
                    pe.matmul(M[:, 1, :], gT[:, P:2 * P], b2_s[:, :], start=True, stop=True).then_inc(m_ready, 1)

            def up_tile(i, e, f):
                kind = "F01" if f < 2 else "F23"
                if f % 2 == 0:
                    pe.wait_ge(w1_in, 16 * (NE * (i - 1) + e + 1))
                    pe.wait_ge(m_taken, piece_no(i, kind, e))
                for k in range(2):
                    last = pe.matmul(M[:, f % 2, :], w1s[:, k, f * P:(f + 1) * P], h2T[:, k, :], start=(k == 0), stop=(k == 1))
                if f % 2 == 1:
                    last.then_inc(m_ready, 1)

            def down_part(i, e, part):
                t, f = part // NF, part % NF
                if part == 0:
                    pe.wait_ge(w2_in, 16 * (NE * (i - 1) + e + 1))
                    pe.wait_ge(m_taken, piece_no(i, "Y", e))
                last = pe.matmul(M[:, t, :], hid[:, f, t * P:(t + 1) * P], w2s[:, f, :], start=(f == 0), stop=(f == NF - 1))
                if part == 2 * NF - 1:
                    last.then_inc(m_ready, 1)

            def scores(i, first, slot, parity):
                n = SLOTS * i + NCHUNK * first + slot
                at_start = isinstance(first, int) and first == 0 and slot < 2
                if due(n - 1 if at_start else n - 2):
                    pe.wait_ge(exp_done, n - 1 if at_start else n - 2)
                tile = first + slot // NCHUNK
                for h in range(2):
                    q0 = (slot % NCHUNK) * CHUNK + h * 512
                    last = pe.matmul(S[score_buffer(first, slot)][:, h, :], kT[parity][:, tile_cols(tile)],
                                     qT[parity][:, q0:q0 + 512], start=True, stop=True)
                last.then_inc(scores_ready, 1)

            def weighted(B, tiles, bset, unit, opens, closes):
                j, half, e = unit // 4, unit // 2 % 2, unit % 2
                if unit <= 1:
                    pe.wait_ge(wsum_ready, B + 1)
                for q in range(4):
                    a0 = ((4 * half + q) * 2 + e) * ROWS
                    last = pe.matmul(R[32 * q:32 * q + 32, half, :], wsum[bset][:, j, 2 * half + q // 2, DH * (1 - e):DH * (3 - e)],
                                     E[bset][j][:, a0:a0 + ROWS], start=(opens and unit == 0),
                                     stop=(closes and j == tiles - 1 and e == 1), skip_group_check=True)
                if unit % 4 == 3:
                    last.then_inc(r_tile_done, 1)

            def add_pool_sum(i):
                pe.wait_ge(pool_steps, POOL_STEPS * i)
                for q in range(4):
                    last = pe.matmul(R[32 * q:32 * q + 32, 0, :], ones_col[:, :], pool_sum[:, q * ROWS:(q + 1) * ROWS],
                                     start=False, stop=False, skip_group_check=True)
                last.then_inc(pool_sum_used, 1)

            pe.wait_ge(c_silu, 1)
            for b in range(NB):
                for n in range(3):
                    at = 3 * b + n
                    for k in range(2):
                        last = pe.matmul(S[at // 2][:, at % 2, :], cwide[:, k, b, :], wmod_s[:, k, n * 512:(n + 1) * 512],
                                         start=(k == 0), stop=(k == 1))
            last.then_inc(mod_ready, 1)
            pe.wait_ge(consts_ready, 1)
            for kind in PRE_PIECES:
                for half in range(1 if kind == "h1T" else 2):
                    pre_piece(-1, kind, half)
            pe.wait_ge(rows_ready, 1)

            PRE_AT = {(1, 5): ("h1T", 0), (1, 6): ("Q", 0), (1, 7): ("Q", 1), (1, 8): ("K", 0), (1, 9): ("K", 1),
                      (2, 3): ("V", 0), (2, 4): ("V", 1)}
            POST_AT = {(1, 2): ("Wo", 0), (1, 3): ("Wo", 1), (1, 11): ("h2T", 0), (2, 1): ("logits", 0),
                       (2, 8): ("gT", 0), (2, 10): ("b2", 0)}
            UNITS = {6: (1, 2), 11: (3, 5, 6)}
            LATE_UNITS = {0: (7, 9), 3: (10, 11)}
            HEAD_UNITS = ({5: (0, 1, 2), 6: (3, 4, 5), 7: (6, 7, 8)},
                          {5: (0, 1), 10: (2, 3), 11: (4, 5)},
                          {5: (0, 1), 6: (2, 3), 7: (4, 5), 9: (6, 8)})
            HEAD_LATE = (LATE_UNITS, {0: (9, 10, 11)}, {0: (6, 7)})
            POOL_SUM_SLOT = 2
            UP_AT = {1: 0, 2: 1, 4: 2, 5: 3}
            DOWN_AT = {7: (0, 1), 8: (2, 3), 9: (4, 5), 10: (6, 7)}

            def pe_block(i, parity, pre, att, post, fin):
                if att:
                    pe.wait_ge(qk_in, 16 * 2 * len(TERMS) * (i + 1))
                for b, (first, tiles) in enumerate(HEAD):
                    B = batch_index(i, b)
                    before = HEAD[b - 1][1] if b > 0 else 3
                    before2 = HEAD[b - 2][1] if b > 1 else 3
                    for slot in range(NCHUNK * tiles):
                        if att:
                            scores(i, first, slot, parity)
                        if (b < 2 and post) or (b == 2 and att):
                            for unit in HEAD_LATE[b].get(slot, ()):
                                weighted(B - 2, before2, set_of(parity, b), unit, False, b == 1)
                        if (b == 0 and post) or (b > 0 and att):
                            if b == 1 and slot == 5 and post:
                                pe.wait_ge(r_taken, i)
                            if b == 0 and slot == POOL_SUM_SLOT:
                                add_pool_sum(i)
                            for unit in HEAD_UNITS[b].get(slot, ()):
                                weighted(B - 1, before, set_of(parity, b - 1), unit, b == 1, False)
                        if post and (b, slot) in POST_AT:
                            post_piece(i, *POST_AT[b, slot], parity)
                        if pre and (b, slot) in PRE_AT:
                            pre_piece(i, *PRE_AT[b, slot])
                if not (att or post):
                    return
                with pe.Fori(0, BODY_ITERS) as it:
                    for h in range(ROUND):
                        b = len(HEAD) + ROUND * it + h
                        B = batch_index(i, b)
                        bset = set_of(parity, len(HEAD) + h)
                        first = BODY_FIRST + 3 * ROUND * it + 3 * h
                        for slot in range(NCHUNK * 3):
                            if att:
                                scores(i, first, slot, parity)
                                for unit in LATE_UNITS.get(slot, ()):
                                    weighted(B - 2, 3, bset, unit, False, False)
                                for unit in UNITS.get(slot, ()):
                                    weighted(B - 1, 3, 1 - bset, unit, False, False)
                            if post and slot in UP_AT:
                                up_tile(i, ROUND * it + h, UP_AT[slot])
                            if post:
                                for part in DOWN_AT.get(slot, ()):
                                    down_part(i, ROUND * it + h, part)

            over_blocks(pe, pe_block)


        @block.scalar
        def _(act):
            def exp_chunk(i, first, slot, b, bset):
                j, ch = slot // NCHUNK, slot % NCHUNK
                if ch == 0:
                    last_use = TILES * i + first + j - (5 if isinstance(b, int) and b > 0 else 6)
                    if due(last_use + 1):
                        act.wait_ge(r_tile_done, last_use + 1)
                    if not isinstance(b, int):
                        act.wait_ge(pool_steps, POOL_STEPS * i + 3 * (b - 3) + j + 1)
                    elif b == 0 and due(i):
                        act.wait_ge(pool_steps, POOL_STEPS * i - 2 + j)
                    elif b == 2 and j == 2 and due(i):
                        act.wait_ge(pool_steps, POOL_STEPS * i)
                act.wait_ge(max_ready, SLOTS * i + NCHUNK * first + slot + 1)
                nc.scalar.activation(E[bset][j][:, ch * CHUNK:(ch + 1) * CHUNK].rearrange("p (h n) -> p h n", h=2),
                                     S[score_buffer(first, slot)][:, :, :], ACT.Exp, bias=nmax[bset][:, j, ch:ch + 1],
                                     accum_out=zc[bset][:, j, ch:ch + 1]).then_inc(exp_done, 1)

            def exp_maxima(B, tiles, bset):
                act.wait_ge(dmax_ready, B + 1)
                nc.scalar.activation(emax[bset][:, 0:tiles, :], dmax[bset][:, 0:tiles, :], ACT.Exp).then_inc(emax_ready, 1)

            def pre_take(i, kind, parity):
                act.wait_ge(m_ready, piece_no(i, kind) + 1)
                if kind == "h1T":
                    last = nc.scalar.activation(h1T[:, :, :], M[:, :, :], ACT.Copy)
                else:
                    if kind != "V":
                        if due(i + 1):
                            act.wait_ge(q_split if kind == "Q" else k_split, i + 1)
                    dst, bias, scale = {"Q": (qf, bq_c, 1.0 / D), "K": (kf, bk_c, 1.0), "V": (vT[parity], bv_c, 1.0)}[kind]
                    for m in range(2):
                        last = nc.scalar.activation(dst[:, m, :], M[:, m, :], ACT.Identity, bias=bias[:, m:m + 1], scale=scale)
                last.then_inc(m_taken, 1)

            def round_part(i, part):
                if part == HI:
                    act.wait_ge(m_taken, piece_no(i, "K") + 1)
                    if due(i + 1):
                        act.wait_ge(k_parts_out, 16 * (i + 1))
                else:
                    act.wait_ge(rest_ready, i + 2)
                nc.scalar.activation(qparts[:, part, :, :], qf[:, :, :], ACT.Copy)
                nc.scalar.activation(kparts[:, part, :, :], kf[:, :, :], ACT.Copy).then_inc(hi_ready if part == HI else mid_ready, 1)

            def post_take(i, kind):
                if kind == "gate exp":
                    act.wait_ge(lgd_ready, i)
                    nc.scalar.activation(lge[:, :, :], lgd[:, :, :], ACT.Exp).then_inc(lge_ready, 1)
                    return
                act.wait_ge(m_ready, piece_no(i, kind) + 1)
                if kind == "h2T":
                    nc.scalar.activation(h2T[:, :, :], M[:, :, :], ACT.Copy).then_inc(m_taken, 1)
                else:
                    nc.scalar.activation(gT[:, :], M[0:NE, 0, :], ACT.Copy).then_inc(m_taken, 1)

            def hidden_take(i, kind, e):
                act.wait_ge(m_ready, piece_no(i, kind, e) + 1)
                for n in range(2):
                    f = (0 if kind == "F01" else 2) + n
                    last = nc.scalar.activation(hid[:, f, :], M[:, n, :], ACT.Relu, bias=b1_c[:, e, f:f + 1])
                last.then_inc(m_taken, 1)

            act.wait_ge(consts_in, 16 * CONST_LOADS)
            nc.scalar.activation(csig, cT, ACT.Exp, scale=-1.0).then_inc(c_exp, 1)
            act.wait_ge(rows_ready, 1)
            for kind in PRE_PIECES:
                pre_take(-1, kind, 0)
            round_part(-1, HI)
            round_part(-1, MID)

            PRE_AT = {(1, 4): "h1T", (1, 6): "Q", (1, 8): "K", (2, 4): "V"}
            ROUND_AT = {(1, 10): HI, (2, 3): MID}
            POST_AT = {(1, 11): "h2T", (2, 2): "gate exp", (2, 7): "gT"}
            EXPERT_AT = {1: "F01", 4: "F23"}

            def act_block(i, parity, pre, att, post, fin):
                for b, (first, tiles) in enumerate(HEAD):
                    for slot in range(NCHUNK * tiles):
                        if att:
                            exp_chunk(i, first, slot, b, set_of(parity, b))
                        if slot == 0 and ((b == 0 and post) or (b > 0 and att)):
                            exp_maxima(batch_index(i, b) - 1, HEAD[b - 1][1] if b > 0 else 3, set_of(parity, b - 1))
                        if post and (b, slot) in POST_AT:
                            post_take(i, POST_AT[b, slot])
                        if pre and (b, slot) in PRE_AT:
                            pre_take(i, PRE_AT[b, slot], 1 - parity)
                        if pre and (b, slot) in ROUND_AT:
                            round_part(i, ROUND_AT[b, slot])
                if not (att or post):
                    return
                with act.Fori(0, BODY_ITERS) as it:
                    for h in range(ROUND):
                        b = len(HEAD) + ROUND * it + h
                        bset = set_of(parity, len(HEAD) + h)
                        for slot in range(NCHUNK * 3):
                            if att:
                                exp_chunk(i, BODY_FIRST + 3 * ROUND * it + 3 * h, slot, b, bset)
                            if att and slot == 0:
                                exp_maxima(batch_index(i, b) - 1, 3, 1 - bset)
                            if post and slot in EXPERT_AT:
                                hidden_take(i, EXPERT_AT[slot], ROUND * it + h)

            over_blocks(act, act_block)

        @block.vector
        def _(dve):
            def chunk_max(i, first, slot, bset):
                n = SLOTS * i + NCHUNK * first + slot + 1
                dve.wait_ge(scores_ready, n)
                dve.tensor_reduce(nmax[bset][:, slot // NCHUNK, slot % NCHUNK:slot % NCHUNK + 1],
                                  S[score_buffer(first, slot)][:, :, :], AX.XY, ALU.max, negate=True).then_inc(max_ready, 1)
                return n

            def all_max(done, tiles, bset):
                dve.wait_ge(max_ready, done)
                dve.tensor_reduce(nall[bset][:, 0:tiles], nmax[bset][:, 0:tiles, :], AX.X, ALU.min).then_inc(nall_ready, 1)

            def max_differences(B, tiles, bset):
                dve.wait_ge(nall_ready, B + 1)
                dve.tensor_tensor(dmax[bset][:, 0:tiles, :], nall[bset][:, 0:tiles].unsqueeze(2).to_broadcast([P, tiles, NCHUNK]),
                                  nmax[bset][:, 0:tiles, :], ALU.subtract).then_inc(dmax_ready, 1)

            def weighted_sums(B, tiles, bset):
                dve.wait_ge(emax_ready, B + 1)
                dve.tensor_tensor(zz[bset][:, 0:tiles, :], zc[bset][:, 0:tiles, :], emax[bset][:, 0:tiles, :], ALU.mult).then_inc(zz_ready, 1)

            def denominators(B, tiles, bset):
                dve.wait_ge(zz_ready, B + 1)
                dve.tensor_reduce(zsum[bset][:, 0:tiles], zz[bset][:, 0:tiles, :], AX.X, ALU.add).then_inc(zsum_ready, 1)
                dve.wait_ge(zsum_ready, B + 1)
                dve.reciprocal(rz[bset][:, 0:tiles], zsum[bset][:, 0:tiles]).then_inc(rz_ready, 1)

            def layer_stats(name, src, n):
                st, mv, _, _ = ln[name]
                bn_done, mean_ready = stats[name][0:2]
                for t in range(2):
                    dve.bn_stats(st[:, t, :], src[:, t, :]).then_inc(bn_done, 1)
                dve.wait_ge(bn_done, 2 * (n + 1))
                on_its_own(dve, 2 * (n + 1))
                for t in range(2):
                    dve.bn_aggr(mv[:, t, :], st[:, t, :]).then_inc(mean_ready, 1)

            def normalise(name, dst, src, n):
                _, mv, _, rs = ln[name]
                dve.wait_ge(stats[name][1], 2 * (n + 1))
                dve.wait_ge(stats[name][3], n + 1)
                for t in range(2):
                    dve.tensor_scalar(dst[:, t, :], src[:, t, :], mv[:, t, 0:1], rs[:, t:t + 1],
                                      ALU.subtract, ALU.mult).then_inc(stats[name][4], 1)

            def residual(i, parity, step):
                if step == "product":
                    if due(i - 1):
                        dve.wait_ge(stored, 16 * (i - 1))
                    dve.wait_ge(m_ready, piece_no(i, "Wo") + 1)
                    dve.tensor_tensor(y[:, :, :], M[:, :, :], rows_of_batch(ga_r, i - 1), ALU.mult).then_inc(m_taken, 1)
                elif step == "sum":
                    dve.wait_ge(m_taken, piece_no(i, "Wo") + 1)
                    dve.wait_ge(x1_biased, i)
                    dve.tensor_tensor(x1[1 - parity][:, :, :], x1[1 - parity][:, :, :], y[:, :, :], ALU.add).then_inc(x1_ready, 1)
                elif step == "statistics":
                    dve.wait_ge(x1_ready, i)
                    layer_stats("two", x1[1 - parity], i - 1)

            def routing(i, step):
                linked = GATE_LINKS * (i - 1)
                if step == "logits":
                    at = piece_no(i, "logits") + 1
                    dve.wait_ge(m_ready, at)
                    dve.tensor_tensor(lg[:, :, :], M[:, :, 0:NE], bg_r[:, :].unsqueeze(1).to_broadcast([P, 2, NE]), ALU.add).then_inc(m_taken, 1)
                    dve.wait_ge(m_taken, at)
                    dve.tensor_reduce(top[:, :], lg[:, :, :], AX.X, ALU.max).then_inc(gate_link, 1)
                elif step == "differences":
                    dve.wait_ge(gate_link, linked + 1)
                    dve.tensor_tensor(lgd[:, :, :], lg[:, :, :], top[:, :].unsqueeze(2).to_broadcast([P, 2, NE]),
                                      ALU.subtract).then_inc(lgd_ready, 1)
                    other = lg[:, :, :].unsqueeze(2).to_broadcast([P, 2, NE, NE])
                    own = lg[:, :, :].unsqueeze(3).to_broadcast([P, 2, NE, NE])
                    dve.tensor_tensor(gt[:, :, :, :], other, own, ALU.is_gt)
                    dve.tensor_tensor(eq[:, :, :, :], other, own, ALU.is_equal).then_inc(gate_link, 1)
                elif step == "ties":
                    before = earlier[:, :, :].unsqueeze(1).to_broadcast([P, 2, NE, NE])
                    dve.wait_ge(gate_link, linked + 2)
                    dve.tensor_tensor(eq[:, :, :, :], eq[:, :, :, :], before, ALU.mult).then_inc(gate_link, 1)
                    dve.wait_ge(gate_link, linked + 3)
                    dve.tensor_tensor(gt[:, :, :, :], gt[:, :, :, :], eq[:, :, :, :], ALU.add).then_inc(gate_link, 1)
                elif step == "rank":
                    dve.wait_ge(gate_link, linked + 4)
                    dve.tensor_reduce(rank[:, :, :], gt[:, :, :, :], AX.X, ALU.add).then_inc(gate_link, 1)
                    dve.wait_ge(gate_link, linked + 5)
                    dve.wait_ge(lge_ready, i)
                    dve.scalar_tensor_tensor(chosen[:, :, :], rank[:, :, :], 1.5, lge[:, :, :], ALU.is_lt, ALU.mult).then_inc(gate_link, 1)
                elif step == "sum":
                    dve.wait_ge(gate_link, linked + 6)
                    dve.tensor_reduce(gsum[:, :], chosen[:, :, :], AX.X, ALU.add).then_inc(gate_link, 1)
                    dve.wait_ge(gate_link, linked + 7)
                    dve.reciprocal(grec[:, :], gsum[:, :]).then_inc(gate_link, 1)
                elif step == "gate":
                    dve.wait_ge(gate_link, linked + 8)
                    dve.tensor_tensor(gate[:, :, :], chosen[:, :, :], grec[:, :].unsqueeze(2).to_broadcast([P, 2, NE]),
                                      ALU.mult).then_inc(gate_ready, 1)

            def start_y(i):
                dve.wait_ge(m_ready, piece_no(i, "b2") + 1)
                dve.tensor_tensor(y[:, :, :], M[:, :, :], h2[:, :, :], ALU.add).then_inc(m_taken, 1)

            def add_expert(i, e):
                at = piece_no(i, "Y", e) + 1
                dve.wait_ge(m_taken, at - 3 if not isinstance(e, int) else at - 1)
                dve.wait_ge(m_ready, at)
                for t in range(2):
                    last = dve.scalar_tensor_tensor(y[:, t, :], M[:, t, :], gate[:, t, bass.ds(e, 1)], y[:, t, :], ALU.mult, ALU.add)
                last.then_inc(m_taken, 1)

            link = Chain(dve, c_link, 0)
            dve.wait_ge(c_exp, 1)
            link(dve.tensor_scalar(csig, csig, 1.0, None, ALU.add))
            link(dve.reciprocal(csil, csig))
            link(dve.tensor_tensor(csil, csil, cT, ALU.mult))
            for k in range(2):
                for b in range(NB):
                    last = dve.tensor_copy(cwide[:, k, b, :], csil[:, k, b:b + 1].to_broadcast([P, P]))
            last.then_inc(c_silu, 1)
            dve.wait_ge(x_in, 16)
            layer_stats("one", xin, 0)
            dve.wait_ge(mod_ready, 1)
            link = Chain(dve, mod_link, 0)
            for b in range(NB):
                for n in range(3):
                    at = 3 * b + n
                    last = dve.tensor_copy(modr[b][:, n * 512:(n + 1) * 512], S[at // 2][:, at % 2, :])
            link(last)
            for b in range(NB):
                part = [modr[b][:, n * D:(n + 1) * D] for n in range(6)]
                dve.tensor_copy(sa_r[:, b, :], part[0])
                dve.tensor_scalar(c1a_r[:, b, :], part[1], 1.0, None, ALU.add)
                dve.tensor_copy(sb_r[:, b, :], part[3])
                dve.tensor_scalar(c1b_r[:, b, :], part[4], 1.0, None, ALU.add)
                for g, at in ((part[2], 0), (part[5], 1)):
                    link(dve.tensor_scalar(scr[:, at, :], g, -1.0, None, ALU.mult))
                    link(dve.tensor_tensor(scr[:, at, :], scr[:, at, :], g, ALU.max))
                    link(dve.tensor_scalar(scr[:, at, :], scr[:, at, :], 0.25, None, ALU.max))
                    link(dve.tensor_scalar(scr2[:, at, :], g, 0.0, 2.0, ALU.is_ge, ALU.mult))
                    link(dve.tensor_scalar(scr2[:, at, :], scr2[:, at, :], -1.0, None, ALU.add))
                    link(dve.tensor_tensor(scr3[:, at, :], scr[:, at, :], scr2[:, at, :], ALU.mult))
                dve.tensor_copy(ga_r[:, b, :], scr3[:, 0, :])
                dve.tensor_tensor(gabo_r[:, b, :], scr3[:, 0, :], bo_r, ALU.mult)
                dve.tensor_tensor(gscale_r[:, b, :], scr3[:, 1, :], gamma_r, ALU.mult)
                link(dve.tensor_tensor(gshift_r[:, b, :], scr3[:, 1, :], beta_r, ALU.mult))
            dve.tensor_scalar(bq_c[:, :], bq_c[:, :], 1.0 / D, None, ALU.mult).then_inc(rows_ready, 1)

            CLOSE_AT = {0: max_differences, 2: weighted_sums, 3: denominators}
            RESIDUAL_AT = {(1, 3): "product", (1, 4): "sum", (1, 5): "statistics"}
            ROUTING_AT = {(2, 1): "logits", (2, 2): "differences", (2, 3): "ties", (2, 4): "rank", (2, 5): "sum", (2, 6): "gate"}

            def dve_block(i, parity, pre, att, post, fin):
                for b, (first, tiles) in enumerate(HEAD):
                    prev = 3 if b == 0 else HEAD[b - 1][1]
                    done = 0
                    for slot in range(NCHUNK * tiles):
                        if att:
                            done = chunk_max(i, first, slot, set_of(parity, b))
                        if slot in CLOSE_AT and ((b == 0 and post) or (b > 0 and att)):
                            CLOSE_AT[slot](batch_index(i, b) - 1, prev, set_of(parity, b - 1))
                        if fin and (b, slot) == (0, 0):
                            dve.wait_ge(m_taken, piece_no(i - 1, "Y", NE - 1) + 1)
                            layer_stats("out", y, i - 2)
                        if pre and (b, slot) == (0, 4):
                            dve.wait_ge(x_in, 16 * (i + 2))
                            layer_stats("one", xin, i + 1)
                        if post and (b, slot) == (1, 0):
                            dve.wait_ge(r_tile_done, TILES * i)
                            dve.tensor_tensor(vT[1 - parity][:, :, :], R[:, :, :], vT[1 - parity][:, :, :], ALU.mult).then_inc(r_taken, 1)
                        if post and (b, slot) in RESIDUAL_AT:
                            residual(i, parity, RESIDUAL_AT[b, slot])
                        if post and (b, slot) == (1, 6):
                            normalise("two", h2, x1[1 - parity], i - 1)
                        if post and (b, slot) in ROUTING_AT:
                            routing(i, ROUTING_AT[b, slot])
                        if post and (b, slot) == (2, 10):
                            start_y(i)
                    if att:
                        all_max(done, tiles, set_of(parity, b))
                if not (att or post):
                    return
                with dve.Fori(0, BODY_ITERS) as it:
                    for h in range(ROUND):
                        b = len(HEAD) + ROUND * it + h
                        bset = set_of(parity, len(HEAD) + h)
                        done = 0
                        for slot in range(NCHUNK * 3):
                            if att:
                                done = chunk_max(i, BODY_FIRST + 3 * ROUND * it + 3 * h, slot, bset)
                            if att and slot in CLOSE_AT:
                                CLOSE_AT[slot](batch_index(i, b) - 1, 3, 1 - bset)
                            if post and slot == 11:
                                add_expert(i, ROUND * it + h)
                        if att:
                            all_max(done, 3, bset)

            over_blocks(dve, dve_block)

        @block.gpsimd
        def _(pool):
            def weights(B, first, tiles, bset):
                pool.wait_ge(rz_ready, B + 1)
                if due(first - 3):
                    pool.wait_ge(r_tile_done, first - 3)
                pool.tensor_tensor(wsum[bset][:, 0:tiles, :, DH:2 * DH],
                                   emax[bset][:, 0:tiles, :].unsqueeze(3).to_broadcast([P, tiles, NCHUNK, DH]),
                                   rz[bset][:, 0:tiles].unsqueeze(2).unsqueeze(3).to_broadcast([P, tiles, NCHUNK, DH]),
                                   ALU.mult).then_inc(wsum_ready, 1)

            def clear_sum(i):
                if due(i):
                    pool.wait_ge(pool_sum_used, i)
                    on_its_own(pool, i)
                pool.memset(pool_sum[:, :], 0.0).then_inc(pool_steps, 3)

            def add_tile(i, n, B, j, bset):
                step = POOL_STEPS * i + 3 + n
                part = E[bset][j][:, 0:2 * QUARTER].rearrange("p (c g e r) -> p c g e r", c=2, g=2, e=2)[:, :, :, 0, :]
                weight = wsum[bset][:, j, 0:2, DH].unsqueeze(2).unsqueeze(3).to_broadcast([P, 2, 2, ROWS])
                sums = pool_sum[:, :].rearrange("p (c g r) -> p c g r", c=2, g=2)
                if j == 0:
                    pool.wait_ge(wsum_ready, B + 1)
                pool.tensor_tensor(part, part, weight, ALU.mult).then_inc(pool_scaled, 1)
                pool.wait_ge(pool_scaled, (POOL_STEPS - 3) * i + n + 1)
                pool.wait_ge(pool_steps, step)
                pool.tensor_tensor(sums, sums, part, ALU.add).then_inc(pool_steps, 1)

            def inverse_deviation(name, n):
                _, mv, ve, rs = ln[name]
                _, mean_ready, ve_ready, rstd_ready, _ = stats[name]
                pool.wait_ge(mean_ready, 2 * (n + 1))
                on_its_own(pool, 2 * (n + 1))
                pool.tensor_scalar(ve[:, :], mv[:, :, 1], EPS, None, ALU.add).then_inc(ve_ready, 1)
                pool.wait_ge(ve_ready, n + 1)
                pool.tensor_tensor(rs[:, :], ve[:, :], mhalf[:, :], ALU.pow).then_inc(rstd_ready, 1)

            def normalise(name, buf, n):
                _, mv, _, rs = ln[name]
                pool.wait_ge(stats[name][3], n + 1)
                on_its_own(pool, n + 1)
                for t in range(2):
                    pool.tensor_scalar(buf[:, t, :], buf[:, t, :], mv[:, t, 0:1], rs[:, t:t + 1],
                                       ALU.subtract, ALU.mult).then_inc(stats[name][4], 1)

            def add_residual(i, parity):
                pool.wait_ge(out_scaled, i - 1)
                pool.wait_ge(x1_shifted, i - 1)
                pool.tensor_tensor(y[:, :, :], y[:, :, :], x1[parity][:, :, :], ALU.add).then_inc(out_ready, 1)

            def scale_rows(name, buf, scale_r, n, scaled):
                pool.wait_ge(stats[name][4], 2 * (n + 1))
                pool.tensor_tensor(buf[:, :, :], buf[:, :, :], rows_of_batch(scale_r, n), ALU.mult).then_inc(scaled, 1)

            def shift_rows(buf, shift_r, n, scaled, ready):
                pool.wait_ge(scaled, n + 1)
                pool.tensor_tensor(buf[:, :, :], buf[:, :, :], rows_of_batch(shift_r, n), ALU.add).then_inc(ready, 1)

            def take_off_high(i):
                pool.wait_ge(hi_ready, i + 2)
                pool.tensor_tensor(qf[:, :, :], qf[:, :, :], qparts[:, HI, :, :], ALU.subtract)
                pool.tensor_tensor(kf[:, :, :], kf[:, :, :], kparts[:, HI, :, :], ALU.subtract).then_inc(rest_ready, 1)

            def low_parts(i):
                pool.wait_ge(mid_ready, i + 2)
                pool.tensor_tensor(qparts[:, LO, :, :], qf[:, :, :], qparts[:, MID, :, :], ALU.subtract).then_inc(q_split, 1)
                pool.tensor_tensor(kparts[:, LO, :, :], kf[:, :, :], kparts[:, MID, :, :], ALU.subtract).then_inc(k_split, 1)

            def bias_residual(i, parity):
                pool.wait_ge(x1_in, 16 * i)
                pool.tensor_tensor(x1[1 - parity][:, :, :], x1[1 - parity][:, :, :], rows_of_batch(gabo_r, i - 1), ALU.add).then_inc(x1_biased, 1)

            def shift_residual(i, parity):
                pool.tensor_tensor(x1[1 - parity][:, :, :], x1[1 - parity][:, :, :], rows_of_batch(gshift_r, i - 1), ALU.add).then_inc(x1_shifted, 1)

            pool.memset(mhalf[:, :], -0.5)
            pool.memset(wsum[0][:, :, :, :], 0.0)
            pool.memset(wsum[1][:, :, :, :], 0.0)
            pool.memset(ones_col[:, :], 0.0)
            pool.memset(earlier[:, :, :], 1.0)
            pool.memset(ident[:, :], 0.0).then_inc(ident_zeroed, 1)
            pool.wait_ge(ident_zeroed, 1)
            pool.affine_select(out=earlier[:, :, :], in_=earlier[:, :, :], compare_op=ALU.is_gt, fill=0.0, base=0,
                               pattern=[[1, NE], [-1, NE]], channel_multiplier=0)
            pool.memset(ones_col[:, 0:DH], 1.0)
            pool.affine_select(out=ident[:, :], in_=ident[:, :], compare_op=ALU.not_equal, fill=1.0, base=0,
                               pattern=[[-1, P]], channel_multiplier=1).then_inc(consts_ready, 1)
            pool.wait_ge(consts_ready, 1)
            inverse_deviation("one", 0)
            normalise("one", xin, 0)
            pool.wait_ge(rows_ready, 1)
            scale_rows("one", xin, c1a_r, 0, h1_scaled)
            shift_rows(xin, sa_r, 0, h1_scaled, h1_ready)
            take_off_high(-1)
            low_parts(-1)

            def pool_block(i, parity, pre, att, post, fin):
                for b, (first, tiles) in enumerate(HEAD):
                    before = HEAD[b - 1][1] if b > 0 else 3
                    B = batch_index(i, b)
                    weigh = (b == 0 and post) or (b > 0 and att)
                    if b == 0 and fin:
                        inverse_deviation("out", i - 2)
                    if b == 2 and pre:
                        take_off_high(i)
                    if weigh:
                        weights(B - 1, TILES * i + first - before, before, set_of(parity, b - 1))
                    if b == 0 and fin:
                        normalise("out", y, i - 2)
                        scale_rows("out", y, gscale_r, i - 2, out_scaled)
                        add_residual(i, parity)
                    if b == 0 and pre:
                        inverse_deviation("one", i + 1)
                        normalise("one", xin, i + 1)
                        scale_rows("one", xin, c1a_r, i + 1, h1_scaled)
                        shift_rows(xin, sa_r, i + 1, h1_scaled, h1_ready)
                    if b == 0 and post:
                        bias_residual(i, parity)
                    if b == 1 and post:
                        inverse_deviation("two", i - 1)
                        scale_rows("two", h2, c1b_r, i - 1, h2_scaled)
                        shift_rows(h2, sb_r, i - 1, h2_scaled, h2_ready)
                        shift_residual(i, parity)
                    if b == 2 and pre:
                        low_parts(i)
                    if b == 1 and att:
                        clear_sum(i)
                if att:
                    with pool.Fori(0, BODY_ITERS) as it:
                        for h in range(ROUND):
                            b = len(HEAD) + ROUND * it + h
                            bset = set_of(parity, len(HEAD) + h)
                            weights(batch_index(i, b) - 1, TILES * i + BODY_FIRST + 3 * ROUND * it + 3 * h - 3, 3, 1 - bset)
                            for j in range(3):
                                add_tile(i, 3 * (ROUND * it + h) + j, batch_index(i, b) - 1, j, 1 - bset)

            over_blocks(pool, pool_block)


_INS = ['L0_attn_X_embed', 'L0_attn_Wq', 'L0_attn_bq', 'L0_attn_Wk', 'L0_attn_bk', 'L0_attn_Wv', 'L0_attn_bv', 'L0_attn_Wo', 'L0_attn_bo', 'L0_ffn_Wg', 'L0_ffn_bg', 'L0_ffn_W1', 'L0_ffn_b1', 'L0_ffn_W2', 'L0_ffn_b2', 'L0_ffn_gamma', 'L0_ffn_beta', 'L0_c', 'L0_wmod']
_OUT = ((2, 4096, 256), "float32")


def kernel(**inputs):
    import numpy as _np
    import concourse.bacc as _bacc
    from concourse import mybir as _mybir
    from concourse.bass_utils import run_bass_kernel_spmd as _run

    nc = _bacc.Bacc("TRN2", target_bir_lowering=False, num_devices=1)
    arrays, args = {}, []
    for name in _INS:
        a = _np.ascontiguousarray(inputs[name])
        arrays[f"in_{name}"] = a
        args.append(nc.dram_tensor(f"in_{name}", a.shape, _mybir.dt.from_np(a.dtype), kind="ExternalInput").ap())
    out = nc.dram_tensor("out", _OUT[0], _mybir.dt.from_np(_np.dtype(_OUT[1])), kind="ExternalOutput").ap()
    adaln_layer(nc, *args, out)
    r = _run(nc, [arrays], core_ids=[0])
    return r.results[0]["out"]
```
